# Optimizing a Trainium2 kernel written in Bass

```python
import numpy as np
import jax
import jax.numpy as jnp

def _softmax(x, axis=-1):
    return jax.nn.softmax(x, axis=axis)

def _gelu(x):
    return jax.nn.gelu(x, approximate=True)

def _silu(x):
    return jax.nn.silu(x)

def _sigmoid(x):
    return jax.nn.sigmoid(x)

def _layernorm(x, axis=-1, eps=1e-05):
    m = jnp.mean(x, axis=axis, keepdims=True)
    v = jnp.var(x, axis=axis, keepdims=True)
    return (x - m) / jnp.sqrt(v + eps)

def _scatter_add(tgt, idx, src, axis=0):
    return tgt.at[idx].add(src)

def _segment_sum(src, seg, n):
    return jax.ops.segment_sum(src, seg, n)
kernel_name = 'mk_dlrm_tower_d1_rec_r8_ad249d'

def setup_inputs(seed: int=0):
    np.random.seed(seed)
    _w = jnp.asarray

    def _rec_inputs():
        import jax
        import jax.numpy as jnp
        _tk = jax.random.key(seed)
        dense_ctx = jax.random.normal(jax.random.fold_in(_tk, 190), (512, 16), jnp.float32)
        ids = jnp.stack([jax.random.randint(jax.random.fold_in(_tk, 200 + f), (512,), 0, v, jnp.int32) for f, v in enumerate([1000, 1250, 1250, 1250, 12500, 12500, 125000, 1000, 1000, 12500, 125000, 1000, 1250, 12500, 1000, 12500, 1000, 12500, 12500, 1000, 125000, 1000, 12500, 125000, 1000, 125000, 12500, 125000, 125000, 1250, 125000, 1000, 1000, 1000, 12500, 12500, 125000, 125000, 12500])], axis=1)
        tbl_0 = 0.05 * jax.random.normal(jax.random.fold_in(_tk, 500 + 0), (1000, 16), jnp.float32)
        tbl_1 = 0.05 * jax.random.normal(jax.random.fold_in(_tk, 500 + 1), (1250, 16), jnp.float32)
        tbl_2 = 0.05 * jax.random.normal(jax.random.fold_in(_tk, 500 + 2), (1250, 16), jnp.float32)
        tbl_3 = 0.05 * jax.random.normal(jax.random.fold_in(_tk, 500 + 3), (1250, 16), jnp.float32)
        tbl_4 = 0.05 * jax.random.normal(jax.random.fold_in(_tk, 500 + 4), (12500, 16), jnp.float32)
        tbl_5 = 0.05 * jax.random.normal(jax.random.fold_in(_tk, 500 + 5), (12500, 16), jnp.float32)
        tbl_6 = 0.05 * jax.random.normal(jax.random.fold_in(_tk, 500 + 6), (125000, 16), jnp.float32)
        tbl_7 = 0.05 * jax.random.normal(jax.random.fold_in(_tk, 500 + 7), (1000, 16), jnp.float32)
        tbl_8 = 0.05 * jax.random.normal(jax.random.fold_in(_tk, 500 + 8), (1000, 16), jnp.float32)
        tbl_9 = 0.05 * jax.random.normal(jax.random.fold_in(_tk, 500 + 9), (12500, 16), jnp.float32)
        tbl_10 = 0.05 * jax.random.normal(jax.random.fold_in(_tk, 500 + 10), (125000, 16), jnp.float32)
        tbl_11 = 0.05 * jax.random.normal(jax.random.fold_in(_tk, 500 + 11), (1000, 16), jnp.float32)
        tbl_12 = 0.05 * jax.random.normal(jax.random.fold_in(_tk, 500 + 12), (1250, 16), jnp.float32)
        tbl_13 = 0.05 * jax.random.normal(jax.random.fold_in(_tk, 500 + 13), (12500, 16), jnp.float32)
        tbl_14 = 0.05 * jax.random.normal(jax.random.fold_in(_tk, 500 + 14), (1000, 16), jnp.float32)
        tbl_15 = 0.05 * jax.random.normal(jax.random.fold_in(_tk, 500 + 15), (12500, 16), jnp.float32)
        tbl_16 = 0.05 * jax.random.normal(jax.random.fold_in(_tk, 500 + 16), (1000, 16), jnp.float32)
        tbl_17 = 0.05 * jax.random.normal(jax.random.fold_in(_tk, 500 + 17), (12500, 16), jnp.float32)
        tbl_18 = 0.05 * jax.random.normal(jax.random.fold_in(_tk, 500 + 18), (12500, 16), jnp.float32)
        tbl_19 = 0.05 * jax.random.normal(jax.random.fold_in(_tk, 500 + 19), (1000, 16), jnp.float32)
        tbl_20 = 0.05 * jax.random.normal(jax.random.fold_in(_tk, 500 + 20), (125000, 16), jnp.float32)
        tbl_21 = 0.05 * jax.random.normal(jax.random.fold_in(_tk, 500 + 21), (1000, 16), jnp.float32)
        tbl_22 = 0.05 * jax.random.normal(jax.random.fold_in(_tk, 500 + 22), (12500, 16), jnp.float32)
        tbl_23 = 0.05 * jax.random.normal(jax.random.fold_in(_tk, 500 + 23), (125000, 16), jnp.float32)
        tbl_24 = 0.05 * jax.random.normal(jax.random.fold_in(_tk, 500 + 24), (1000, 16), jnp.float32)
        tbl_25 = 0.05 * jax.random.normal(jax.random.fold_in(_tk, 500 + 25), (125000, 16), jnp.float32)
        tbl_26 = 0.05 * jax.random.normal(jax.random.fold_in(_tk, 500 + 26), (12500, 16), jnp.float32)
        tbl_27 = 0.05 * jax.random.normal(jax.random.fold_in(_tk, 500 + 27), (125000, 16), jnp.float32)
        tbl_28 = 0.05 * jax.random.normal(jax.random.fold_in(_tk, 500 + 28), (125000, 16), jnp.float32)
        tbl_29 = 0.05 * jax.random.normal(jax.random.fold_in(_tk, 500 + 29), (1250, 16), jnp.float32)
        tbl_30 = 0.05 * jax.random.normal(jax.random.fold_in(_tk, 500 + 30), (125000, 16), jnp.float32)
        tbl_31 = 0.05 * jax.random.normal(jax.random.fold_in(_tk, 500 + 31), (1000, 16), jnp.float32)
        tbl_32 = 0.05 * jax.random.normal(jax.random.fold_in(_tk, 500 + 32), (1000, 16), jnp.float32)
        tbl_33 = 0.05 * jax.random.normal(jax.random.fold_in(_tk, 500 + 33), (1000, 16), jnp.float32)
        tbl_34 = 0.05 * jax.random.normal(jax.random.fold_in(_tk, 500 + 34), (12500, 16), jnp.float32)
        tbl_35 = 0.05 * jax.random.normal(jax.random.fold_in(_tk, 500 + 35), (12500, 16), jnp.float32)
        tbl_36 = 0.05 * jax.random.normal(jax.random.fold_in(_tk, 500 + 36), (125000, 16), jnp.float32)
        tbl_37 = 0.05 * jax.random.normal(jax.random.fold_in(_tk, 500 + 37), (125000, 16), jnp.float32)
        tbl_38 = 0.05 * jax.random.normal(jax.random.fold_in(_tk, 500 + 38), (12500, 16), jnp.float32)
        _rk = jax.random.fold_in(_tk, 7)
        W_top1 = 0.05 * jax.random.normal(jax.random.fold_in(_tk, 801), (400, 512), jnp.float32)
        W_top2 = 0.0441942 * jax.random.normal(jax.random.fold_in(_tk, 802), (512, 256), jnp.float32)
        W_top3 = 0.0625 * jax.random.normal(jax.random.fold_in(_tk, 803), (256, 1), jnp.float32)
        b_top1 = jnp.zeros((512,), jnp.float32)
        b_top2 = jnp.zeros((256,), jnp.float32)
        return (dense_ctx, ids, tbl_0, tbl_1, tbl_2, tbl_3, tbl_4, tbl_5, tbl_6, tbl_7, tbl_8, tbl_9, tbl_10, tbl_11, tbl_12, tbl_13, tbl_14, tbl_15, tbl_16, tbl_17, tbl_18, tbl_19, tbl_20, tbl_21, tbl_22, tbl_23, tbl_24, tbl_25, tbl_26, tbl_27, tbl_28, tbl_29, tbl_30, tbl_31, tbl_32, tbl_33, tbl_34, tbl_35, tbl_36, tbl_37, tbl_38, W_top1, b_top1, W_top2, b_top2, W_top3)
    dense_ctx, ids, tbl_0, tbl_1, tbl_2, tbl_3, tbl_4, tbl_5, tbl_6, tbl_7, tbl_8, tbl_9, tbl_10, tbl_11, tbl_12, tbl_13, tbl_14, tbl_15, tbl_16, tbl_17, tbl_18, tbl_19, tbl_20, tbl_21, tbl_22, tbl_23, tbl_24, tbl_25, tbl_26, tbl_27, tbl_28, tbl_29, tbl_30, tbl_31, tbl_32, tbl_33, tbl_34, tbl_35, tbl_36, tbl_37, tbl_38, W_top1, b_top1, W_top2, b_top2, W_top3 = _rec_inputs()

    def _L0_rec_setup():
        import jax, jax.numpy as jnp
        import numpy as np
        B, F0, D = (256, 39, 16)
        CROSS = [128, 128, 128]
        key = jax.random.key(seed)
        k0, k1, k2, k3 = jax.random.split(key, 4)
        inputs = jax.random.normal(k0, (B, F0, D), dtype=jnp.float32)
        f0 = jax.random.normal(k1, (F0 * F0, CROSS[0]), dtype=jnp.float32) * 0.05
        f1 = jax.random.normal(k2, (CROSS[0] * F0, CROSS[1]), dtype=jnp.float32) * 0.05
        f2 = jax.random.normal(k3, (CROSS[1] * F0, CROSS[2]), dtype=jnp.float32) * 0.05
        return {'inputs': inputs, 'f0': f0, 'f1': f1, 'f2': f2}
    _L0_rec_all = _L0_rec_setup()
    _L0_rec_in = {k: v for k, v in _L0_rec_all.items() if k in ('f0', 'f1', 'f2')}
    del _L0_rec_all
    return {'dense_ctx': dense_ctx, 'ids': ids, 'tbl_0': tbl_0, 'tbl_1': tbl_1, 'tbl_2': tbl_2, 'tbl_3': tbl_3, 'tbl_4': tbl_4, 'tbl_5': tbl_5, 'tbl_6': tbl_6, 'tbl_7': tbl_7, 'tbl_8': tbl_8, 'tbl_9': tbl_9, 'tbl_10': tbl_10, 'tbl_11': tbl_11, 'tbl_12': tbl_12, 'tbl_13': tbl_13, 'tbl_14': tbl_14, 'tbl_15': tbl_15, 'tbl_16': tbl_16, 'tbl_17': tbl_17, 'tbl_18': tbl_18, 'tbl_19': tbl_19, 'tbl_20': tbl_20, 'tbl_21': tbl_21, 'tbl_22': tbl_22, 'tbl_23': tbl_23, 'tbl_24': tbl_24, 'tbl_25': tbl_25, 'tbl_26': tbl_26, 'tbl_27': tbl_27, 'tbl_28': tbl_28, 'tbl_29': tbl_29, 'tbl_30': tbl_30, 'tbl_31': tbl_31, 'tbl_32': tbl_32, 'tbl_33': tbl_33, 'tbl_34': tbl_34, 'tbl_35': tbl_35, 'tbl_36': tbl_36, 'tbl_37': tbl_37, 'tbl_38': tbl_38, 'W_top1': W_top1, 'b_top1': b_top1, 'W_top2': W_top2, 'b_top2': b_top2, 'W_top3': W_top3, 'L0_rec_f0': _L0_rec_in['f0'], 'L0_rec_f1': _L0_rec_in['f1'], 'L0_rec_f2': _L0_rec_in['f2']}

def reference(dense_ctx, ids, tbl_0, tbl_1, tbl_2, tbl_3, tbl_4, tbl_5, tbl_6, tbl_7, tbl_8, tbl_9, tbl_10, tbl_11, tbl_12, tbl_13, tbl_14, tbl_15, tbl_16, tbl_17, tbl_18, tbl_19, tbl_20, tbl_21, tbl_22, tbl_23, tbl_24, tbl_25, tbl_26, tbl_27, tbl_28, tbl_29, tbl_30, tbl_31, tbl_32, tbl_33, tbl_34, tbl_35, tbl_36, tbl_37, tbl_38, W_top1, b_top1, W_top2, b_top2, W_top3, L0_rec_f0, L0_rec_f1, L0_rec_f2):
    import jax
    import jax.numpy as jnp

    def _L0_rec_ref(inputs, f0, f1, f2):
        import jax, jax.numpy as jnp
        import numpy as np
        B, F0, D = (256, 39, 16)
        CROSS = [128, 128, 128]
        filters = [f0, f1, f2]
        x0 = inputs
        xk = inputs
        outs = []
        for W in filters:
            b, f, d = x0.shape
            g = xk.shape[1]
            z = jnp.einsum('bfd,bgd->bfgd', x0, xk).reshape(b, f * g, d)
            cur = jnp.einsum('bpd,pm->bmd', z, W)
            outs.append(cur)
            xk = cur
        result = jnp.concatenate(outs, axis=1)
        return jnp.sum(result, axis=-1)
    e = jnp.stack([tbl_0[ids[:, 0]], tbl_1[ids[:, 1]], tbl_2[ids[:, 2]], tbl_3[ids[:, 3]], tbl_4[ids[:, 4]], tbl_5[ids[:, 5]], tbl_6[ids[:, 6]], tbl_7[ids[:, 7]], tbl_8[ids[:, 8]], tbl_9[ids[:, 9]], tbl_10[ids[:, 10]], tbl_11[ids[:, 11]], tbl_12[ids[:, 12]], tbl_13[ids[:, 13]], tbl_14[ids[:, 14]], tbl_15[ids[:, 15]], tbl_16[ids[:, 16]], tbl_17[ids[:, 17]], tbl_18[ids[:, 18]], tbl_19[ids[:, 19]], tbl_20[ids[:, 20]], tbl_21[ids[:, 21]], tbl_22[ids[:, 22]], tbl_23[ids[:, 23]], tbl_24[ids[:, 24]], tbl_25[ids[:, 25]], tbl_26[ids[:, 26]], tbl_27[ids[:, 27]], tbl_28[ids[:, 28]], tbl_29[ids[:, 29]], tbl_30[ids[:, 30]], tbl_31[ids[:, 31]], tbl_32[ids[:, 32]], tbl_33[ids[:, 33]], tbl_34[ids[:, 34]], tbl_35[ids[:, 35]], tbl_36[ids[:, 36]], tbl_37[ids[:, 37]], tbl_38[ids[:, 38]]], axis=1)
    z = _L0_rec_ref(e, L0_rec_f0, L0_rec_f1, L0_rec_f2)
    z = z.reshape(z.shape[0], -1)
    h = jnp.concatenate([z, dense_ctx], axis=1)
    h = jnp.maximum(h @ W_top1 + b_top1, 0.0)
    h = jnp.maximum(h @ W_top2 + b_top2, 0.0)
    y = h @ W_top3
    return y

_drawn_inputs = setup_inputs


def setup_inputs(seed=0):
    import zlib

    import numpy as np

    out = dict(_drawn_inputs(seed))
    spreads = {'b_top1': (0.0, 0.586), 'b_top2': (0.0, 0.1)}
    factors = {'tbl_0': 4.465,
     'tbl_1': 5.157,
     'tbl_2': 4.69,
     'tbl_3': 4.831,
     'tbl_4': 4.785,
     'tbl_5': 4.99,
     'tbl_6': 4.453,
     'tbl_7': 4.655,
     'tbl_8': 5.021,
     'tbl_9': 4.594,
     'tbl_10': 4.89,
     'tbl_11': 4.736,
     'tbl_12': 4.361,
     'tbl_13': 4.266,
     'tbl_14': 4.722,
     'tbl_15': 4.883,
     'tbl_16': 5.204,
     'tbl_17': 4.89,
     'tbl_18': 5.016,
     'tbl_19': 4.581,
     'tbl_20': 5.102,
     'tbl_21': 4.823,
     'tbl_22': 4.381,
     'tbl_23': 5.137,
     'tbl_24': 4.33,
     'tbl_25': 4.488,
     'tbl_26': 4.835,
     'tbl_27': 4.767,
     'tbl_28': 4.489,
     'tbl_29': 4.806,
     'tbl_30': 5.005,
     'tbl_31': 4.52,
     'tbl_32': 4.811,
     'tbl_33': 4.824,
     'tbl_34': 4.534,
     'tbl_35': 4.757,
     'tbl_36': 4.97,
     'tbl_37': 4.886,
     'tbl_38': 5.263,
     'L0_rec_f1': 5.247,
     'L0_rec_f2': 8.0}
    for name, (base, spread) in spreads.items():
        noise = np.random.default_rng([zlib.crc32(name.encode()), seed]).standard_normal(out[name].shape)
        drawn = base * np.exp(spread * noise) if base else spread * noise
        out[name] = jnp.asarray(drawn.astype(out[name].dtype))
    for name, factor in factors.items():
        out[name] = (out[name] * factor).astype(out[name].dtype)
    return out
```

```python
from contextlib import ExitStack

import concourse.bass as bass
import numpy as np
from concourse import mybir

F32 = mybir.dt.float32
BF16 = mybir.dt.bfloat16
I32 = mybir.dt.int32
ALU = mybir.AluOpType
ACT = mybir.ActivationFunctionType
AX_X = mybir.AxisListType.X

P = 128
BATCH = 512
FIELDS = 39
D = 16
MAPS = 128
PARTS = 3
PF = PARTS * FIELDS
GROUPS = BATCH // P
CB = 32
CHUNKS = BATCH // CB
PER_GROUP = P // CB
N = CB * D
SHIFTS = (FIELDS + 1) // 2
PER_TILE = 3
T0 = -(-SHIFTS // PER_TILE)
FI, GJ = 10, 4
FQ, GQ = P // 32, P // GJ
SB = 8
SUBS = CB // SB
FG = FIELDS + 1
H1, H2 = 512, 256
ITEMS0 = T0 + 2
ITEMS = T0 + 1 + FI


def tile_rows(t):
    return FIELDS * min(PER_TILE, SHIFTS - PER_TILE * t)


def build_program(nc, a):
    w1_rows = a["L0_rec_f1"].rearrange("(f q j) m -> f q (j m)", f=FIELDS, j=GJ)
    w2_rows = a["L0_rec_f2"].rearrange("(f g) m -> g f m", f=FIELDS)
    x1_dram = nc.dram_tensor("x1_dram", [CHUNKS, MAPS, N], F32, kind="Internal").ap()

    with ExitStack() as ctx:
        def sb(name, shape, dt=F32):
            return ctx.enter_context(nc.sbuf_tensor(name, shape, dt))

        def bank(name, shape, dt=F32):
            return ctx.enter_context(nc.psum_tensor(name, shape, dt))

        def sem(name):
            return ctx.enter_context(nc.semaphore(name))

        sel_field = sb("sel_field", [PF, FI, P], BF16)
        sel_shift = sb("sel_shift", [PF, T0 + 1, PER_TILE * FIELDS], BF16)
        sel_sum = sb("sel_sum", [PF, FIELDS], BF16)
        ident_b = sb("ident_b", [P, P], BF16)
        ident = sb("ident", [P, P])
        mask = sb("mask", [P, SB])
        w0 = sb("w0", [PER_TILE * FIELDS, T0, MAPS])
        w1 = sb("w1", [P, FI, GJ, MAPS])
        w2 = sb("w2", [P, FIELDS, MAPS])
        ids = sb("ids_sb", [P, GROUPS, FIELDS], I32)
        emb = sb("emb", [P, 2, FIELDS, D])
        emb_parts = sb("emb_parts", [P, D, PF], BF16)
        x0_parts = sb("x0_parts", [PF, CHUNKS * SUBS, D, SB], BF16)
        x0_thrice = sb("x0_thrice", [PER_TILE * FIELDS, N])
        z0 = sb("z0", [PER_TILE * FIELDS, 2, N])
        x1 = sb("x1", [MAPS, N])
        x1_pat = sb("x1_pat", [P, 2, GJ, N])
        z1 = sb("z1", [P, 2, GJ, N])
        x2 = sb("x2", [MAPS, SUBS, D * SB])
        x2_t = sb("x2_t", [P, SUBS, MAPS])
        x0_diag = sb("x0_diag", [P, SUBS, SB, FG])
        g_sum = sb("g_sum", [MAPS, FG, BATCH])
        out0 = sb("out0", [MAPS, BATCH])
        dense = sb("dense_sb", [P, GROUPS, D])
        dense_t = sb("dense_t", [D, BATCH])
        bias1 = sb("bias1", [P, H1 // P])
        bias2 = sb("bias2", [P, H2 // P])
        wt3 = sb("wt3", [P, H2 // P])
        wt1 = x1_pat[:, 0, 0:3, :]
        wt1_dense = x1_pat[0:D, 0, 3, :]
        wt2 = x1_pat[:, 1, 0:2, :].rearrange("p a (k n) -> p (a k) n", k=2)
        h1 = z1[:, 0, :, :]
        h2 = z1[:, 1, 0:2, :]
        out2 = z1[:, 1, 2, :]
        y = z1[0:1, 1, 3, :]
        w0_mirror = z1[0:PER_TILE * FIELDS, 1, 0:2, :].rearrange("p a (t m) -> p (a t) m", m=MAPS)[:, 0:T0, :]

        pat = bank("pat", [P, 2, N])
        acc1 = bank("acc1", [MAPS, N])
        acc0 = bank("acc0", [MAPS, N])
        x0t_ps = bank("x0t_ps", [P, N])
        x2t_ps = bank("x2t_ps", [P, SUBS, MAPS])
        wide = bank("wide", [P, 2, N])
        x0_t = x0t_ps[:, 0:SUBS * FIELDS].rearrange("p (s f) -> p s f", s=SUBS)
        h1_bank = [pat[:, 0, :], pat[:, 1, :], acc0[:], x0t_ps[:]]
        y_bank = x2t_ps[0:1, :, :].rearrange("o s m -> o (s m)")
        parts_t = wide[:, :, :].bitcast(BF16).rearrange("p a (d b) -> p (a d) b", b=P)

        consts_in = sem("consts_in")
        w0_in = sem("w0_in")
        w1_in = sem("w1_in")
        w2_in = sem("w2_in")
        dense_in = sem("dense_in")
        top_in = sem("top_in")
        small_in = sem("small_in")
        ids_in = sem("ids_in")
        gathered = [sem(f"gathered{n}") for n in range(2)]
        split_step = sem("split_step")
        parts_turned = sem("parts_turned")
        parts_kept = sem("parts_kept")
        w0_ready = sem("w0_ready")
        w1_pad = sem("w1_pad")
        mask_set = sem("mask_set")
        dense_turned = sem("dense_turned")
        dense_kept = sem("dense_kept")
        pat_ready = sem("pat_ready")
        thrice_ready = sem("thrice_ready")
        z0_ready = sem("z0_ready")
        l0_step = sem("l0_step")
        x1_ready = sem("x1_ready")
        x1_stored = sem("x1_stored")
        x1_pat_in = sem("x1_pat_in")
        out0_ready = sem("out0_ready")
        z1_ready = sem("z1_ready")
        l1_step = sem("l1_step")
        x2_ready = sem("x2_ready")
        x2_turned = sem("x2_turned")
        x2t_ready = sem("x2t_ready")
        x0t_ready = sem("x0t_ready")
        diag_ready = sem("diag_ready")
        g_ready = sem("g_ready")
        g_kept = sem("g_kept")
        out2_done = sem("out2_done")
        out2_ready = sem("out2_ready")
        h1_done = sem("h1_done")
        h1_ready = sem("h1_ready")
        h2_done = sem("h2_done")
        h2_ready = sem("h2_ready")
        y_done = sem("y_done")
        y_ready = sem("y_ready")
        y_out = sem("y_out")

        def at_least(eng, s, value):
            if not isinstance(value, int) or value > 0:
                eng.wait_ge(s, value)

        def is_first(c):
            return isinstance(c, int) and c == 0

        def over_chunks(eng, body, prepare):
            body(0, False, 1)
            body(1, False, 1)
            with eng.Fori(0, GROUPS - 1) as t:
                prepare(t + 1)
                with eng.Fori(0, PER_GROUP) as q:
                    body(t * PER_GROUP + q + 2, False, t + 2)
            body(CHUNKS - 2, False, GROUPS)
            body(CHUNKS - 1, True, GROUPS)

        def order(last):
            fields = [("field", i + 1) for i in range(FI - 1 if last else FI)]
            if last:
                return fields
            found = []
            for i, field in enumerate(fields):
                found.append(field)
                if i == 0:
                    found.append(("thrice", 0))
                found += [("shift", t) for t in range(2 * i, min(2 * i + 2, T0))]
            return found

        def pattern_ready(eng, c, last, what):
            n = order(last).index(what)
            at_least(eng, pat_ready, c * ITEMS + ITEMS0 + n + 1)
            return n % 2

        block = ctx.enter_context(nc.Block())

        @block.sync
        def _(sp):
            sp.dma_start(ids[:], a["ids"].rearrange("(t p) f -> p t f", p=P)).then_inc(ids_in, 16)
            for dst, name in ((ident_b, "ident_b"), (sel_shift, "sel_shift"), (sel_field, "sel_field"),
                              (sel_sum, "sel_sum"), (ident, "ident"), (mask, "mask")):
                sp.dma_start(dst[:], a[name]).then_inc(consts_in, 16)
            sp.dma_start(w0[:], a["w0_upper"]).then_inc(w0_in, 16)
            sp.dma_start(w0_mirror, a["w0_lower"]).then_inc(w0_in, 16)
            sp.dma_start(dense[:], a["dense_ctx"].rearrange("(t p) d -> p t d", p=P)).then_inc(dense_in, 16)
            for fq in range(FQ):
                fields = min(FI, FIELDS - FI * fq)
                sp.dma_start(w1[32 * fq:32 * fq + 32, 0:fields, :, :].rearrange("p f j m -> p f (j m)"),
                             w1_rows[FI * fq:FI * fq + fields, :, :].rearrange("f q n -> q f n")).then_inc(w1_in, 16)
            sp.dma_start(w2[:], w2_rows).then_inc(w2_in, 16)
            with nc.allow_non_contiguous_dma(reason="a few hundred words"):
                sp.dma_start(bias1[:], a["b_top1"].rearrange("(k p) -> p k", p=P)).then_inc(small_in, 16)
                sp.dma_start(bias2[:], a["b_top2"].rearrange("(k p) -> p k", p=P)).then_inc(small_in, 16)
                sp.dma_start(wt3[:], a["W_top3"].rearrange("(k p) o -> p (k o)", p=P)).then_inc(small_in, 16)

            def spread(c):
                at_least(sp, x1_ready, c + 1)
                sp.dma_start(x1_dram[c], x1[:]).then_inc(x1_stored, 16)
                at_least(sp, x1_stored, 16 * c + 16)
                if not (isinstance(c, int) and c < 2):
                    at_least(sp, z1_ready, FI * c - FI)
                for fq in range(FQ):
                    sp.dma_start(x1_pat[32 * fq:32 * fq + 32, c % 2, :, :].rearrange("q j n -> q (j n)"),
                                 x1_dram[c].rearrange("(q j) n -> q (j n)", j=GJ)).then_inc(x1_pat_in, 16)

            spread(0)
            spread(1)
            with sp.Fori(2, CHUNKS) as c:
                spread(c)
            sp.wait_ge(z1_ready, FI * CHUNKS)
            sp.dma_start(wt1, a["W_top1"][0:3 * MAPS, :].rearrange("(k p) n -> p k n", p=P)).then_inc(top_in, 16)
            sp.dma_start(wt1_dense, a["W_top1"][3 * MAPS:3 * MAPS + D, :]).then_inc(top_in, 16)
            sp.dma_start(wt2, a["W_top2"].rearrange("(k p) n -> p k n", p=P)).then_inc(top_in, 16)
            sp.wait_ge(y_ready, 1)
            sp.dma_start(a["out"].rearrange("b o -> o b"), y).then_inc(y_out, 16)
            sp.wait_ge(y_out, 16)

        def cut(eng, t):
            value = emb[:, t % 2, :, :].rearrange("p f d -> p d f")
            part = [emb_parts[:, :, FIELDS * k:FIELDS * k + FIELDS] for k in range(PARTS)]
            eng.wait_ge(gathered[t % 2], 16 * FIELDS * (t // 2 + 1))
            if t:
                eng.wait_ge(parts_turned, t)
            eng.tensor_copy(part[0], value).then_inc(split_step, 1)
            eng.wait_ge(split_step, 4 * t + 1)
            eng.tensor_tensor(value, value, part[0], ALU.subtract).then_inc(split_step, 1)
            eng.wait_ge(split_step, 4 * t + 2)
            eng.tensor_copy(part[1], value).then_inc(split_step, 1)
            eng.wait_ge(split_step, 4 * t + 3)
            eng.tensor_tensor(part[2], value, part[1], ALU.subtract).then_inc(split_step, 1)

        @block.gpsimd
        def _(pool):
            def gather(t):
                if t >= 2:
                    pool.wait_ge(split_step, 4 * (t - 1))
                for f in range(FIELDS):
                    pool.indirect_dma_start(
                        out=emb[:, t % 2, f, :], out_offset=None, in_=a[f"tbl_{f}"][:, :],
                        in_offset=bass.IndirectOffsetOnAxis(ap=ids[:, t, f:f + 1], axis=0),
                    ).then_inc(gathered[t % 2], 16)

            pool.wait_ge(ids_in, 16)
            gather(0)
            gather(1)
            for t in range(1, GROUPS):
                if t + 1 < GROUPS:
                    gather(t + 1)
                cut(pool, t)

        @block.vector
        def _(dve):
            dve.memset(w1[32 * (FQ - 1):P, FI - 1, :, :], 0.0).then_inc(w1_pad, 1)
            dve.wait_ge(consts_in, 96)
            dve.tensor_copy(x0_diag[:, :, :, FIELDS], mask[:].rearrange("p (o b) -> p o b", o=1)
                            .to_broadcast([P, SUBS, SB])).then_inc(mask_set, 1)
            dve.wait_ge(w0_in, 32)
            dve.tensor_tensor(w0[:], w0[:], w0_mirror, ALU.add).then_inc(w0_ready, 1)
            dve.wait_ge(dense_turned, 1)
            dve.tensor_copy(dense_t[:], x0t_ps[0:D, :]).then_inc(dense_kept, 1)
            cut(dve, 0)

            def products0(c, t, bank_of):
                rows = tile_rows(t)
                if t == 0:
                    at_least(dve, thrice_ready, c + 1)
                if not (isinstance(c, int) and c == 0 and t < 2):
                    at_least(dve, l0_step, c * T0 + max(t - 1, 0))
                dve.tensor_tensor(z0[0:rows, t % 2, :], pat[0:rows, bank_of, :], x0_thrice[0:rows, :],
                                  ALU.mult).then_inc(z0_ready, 1)

            def products1(c, i, bank_of):
                if i == 0:
                    at_least(dve, x1_pat_in, c * (16 * FQ) + 16 * FQ)
                if not (isinstance(c, int) and c == 0 and i < 2):
                    at_least(dve, l1_step, c * FI + (i - 1))
                dve.tensor_tensor(z1[:, i % 2, :, :], pat[:, bank_of:bank_of + 1, :].to_broadcast([P, GJ, N]),
                                  x1_pat[:, c % 2, :, :], ALU.mult).then_inc(z1_ready, 1)

            def sum_x1(c):
                at_least(dve, x1_ready, c + 1)
                dve.tensor_reduce(out0[:, bass.ds(c * CB, CB)].rearrange("m (s b) -> m s b", s=SUBS),
                                  x1[:].rearrange("m (s d b) -> m s b d", s=SUBS, d=D),
                                  AX_X, ALU.add).then_inc(out0_ready, 1)

            def diagonals(c):
                at_least(dve, x0t_ready, c + 1)
                at_least(dve, g_ready, c * SUBS)
                for s in range(SUBS):
                    dve.tensor_tensor(
                        x0_diag[:, s, :, 0:FIELDS], x0_t[:, s:s + 1, :].to_broadcast([P, SB, FIELDS]),
                        mask[:].rearrange("p (b o) -> p b o", o=1).to_broadcast([P, SB, FIELDS]),
                        ALU.mult).then_inc(diag_ready, 1)

            for t in range(T0):
                dve.wait_ge(pat_ready, t + 2)
                products0(0, t, t % 2)
            sum_x1(0)
            dve.wait_ge(pat_ready, ITEMS0)
            dve.wait_ge(w0_ready, 1)
            products1(0, 0, 1)

            def body(c, last, groups):
                for i in range(FI):
                    if i < FI - 1:
                        products1(c, i + 1, pattern_ready(dve, c, last, ("field", i + 1)))
                    elif not last:
                        products1(c + 1, 0, pattern_ready(dve, c, last, ("field", FI)))
                    if not last:
                        for t in range(2 * i, min(2 * i + 2, T0)):
                            products0(c + 1, t, pattern_ready(dve, c, last, ("shift", t)))
                    if i == 4 and not is_first(c):
                        diagonals(c - 1)
                    if i == 6 and not last:
                        sum_x1(c + 1)

            over_chunks(dve, body, lambda t: None)
            diagonals(CHUNKS - 1)

        @block.scalar
        def _(act):
            def keep_parts(t):
                at_least(act, parts_turned, t + 1)
                act.copy(x0_parts[:, bass.ds(t * (PER_GROUP * SUBS), PER_GROUP * SUBS), :, :],
                         parts_t[0:PF, :, :].rearrange("r d (s b) -> r s d b", b=SB)).then_inc(parts_kept, 1)

            def keep_thrice(c, bank_of):
                at_least(act, z0_ready, c * T0)
                act.copy(x0_thrice[:], pat[0:PER_TILE * FIELDS, bank_of, :]).then_inc(thrice_ready, 1)

            def keep_x1(c):
                at_least(act, l0_step, c * T0 + T0)
                at_least(act, x1_stored, c * 16)
                at_least(act, out0_ready, c)
                act.copy(x1[:], acc0[:]).then_inc(x1_ready, 1)

            def keep_x2(c):
                at_least(act, l1_step, c * FI + FI)
                at_least(act, x2_turned, c)
                act.copy(x2[:], acc1[:].rearrange("m (s n) -> m s n", s=SUBS)).then_inc(x2_ready, 1)

            def keep_x2_t(c):
                at_least(act, x2_turned, c + 1)
                at_least(act, g_ready, c * SUBS)
                act.copy(x2_t[:], x2t_ps[:]).then_inc(x2t_ready, 1)

            def keep_g(c):
                for s in range(SUBS):
                    at_least(act, g_ready, c * SUBS + s + 1)
                    act.copy(g_sum[:, :, bass.ds(c * CB + s * SB, SB)],
                             wide[:, s % 2, 0:SB * FG].rearrange("g (b f) -> g f b", b=SB)).then_inc(g_kept, 1)

            keep_parts(0)
            act.wait_ge(pat_ready, 1)
            keep_thrice(0, 1)
            keep_x1(0)

            def body(c, last, groups):
                if not is_first(c):
                    keep_x2(c - 1)
                if not last:
                    keep_thrice(c + 1, pattern_ready(act, c, last, ("thrice", 0)))
                    keep_x1(c + 1)
                if not is_first(c):
                    keep_x2_t(c - 1)
                    keep_g(c - 1)

            over_chunks(act, body, keep_parts)
            keep_x2(CHUNKS - 1)
            keep_x2_t(CHUNKS - 1)
            keep_g(CHUNKS - 1)
            act.wait_ge(out2_done, 1)
            act.copy(out2, acc1[:]).then_inc(out2_ready, 1)
            act.wait_ge(small_in, 48)
            for m in range(H1 // P):
                act.wait_ge(h1_done, m + 1)
                act.activation(h1[:, m, :], h1_bank[m], ACT.Relu, bias=bias1[:, m:m + 1]).then_inc(h1_ready, 1)
            for m in range(H2 // P):
                act.wait_ge(h2_done, m + 1)
                act.activation(h2[:, m, :], wide[:, m, :], ACT.Relu, bias=bias2[:, m:m + 1]).then_inc(h2_ready, 1)
            act.wait_ge(y_done, 1)
            act.copy(y, y_bank).then_inc(y_ready, 1)

        @block.tensor
        def _(pe):
            def turn_parts(t):
                at_least(pe, split_step, t * 4 + 4)
                at_least(pe, g_kept, t * (PER_GROUP * SUBS) - (PER_GROUP - 1) * SUBS)
                for d in range(D):
                    last = pe.transpose(parts_t[0:PF, d, :], emb_parts[:, d, :], ident_b[:])
                last.then_inc(parts_turned, 1)

            def parts(c):
                return x0_parts[:, bass.ds(c * SUBS, SUBS), :, :].rearrange("r s d b -> r (s d b)")

            def pattern(sel, c, bank_of):
                pe.matmul(pat[0:sel.shape[1], bank_of, :], sel, parts(c), start=True, stop=True).then_inc(pat_ready, 1)

            def body_pattern(c, last, what):
                n = order(last).index(what)
                if n >= 2:
                    before, k = order(last)[n - 2]
                    if before == "field":
                        at_least(pe, z1_ready, c * FI + k + 1)
                    elif before == "thrice":
                        at_least(pe, thrice_ready, c + 2)
                    else:
                        at_least(pe, z0_ready, c * T0 + (T0 + k + 1))
                elif n == 1 or not is_first(c):
                    at_least(pe, z1_ready, c * FI + n)
                else:
                    pe.wait_ge(z0_ready, T0)
                kind, k = what
                if kind == "field":
                    pattern(sel_field[:, k % FI, :], c + 1 if k == FI else c, n % 2)
                elif kind == "thrice":
                    pattern(sel_shift[:, T0, :], c + 1, n % 2)
                else:
                    pattern(sel_shift[:, k, 0:tile_rows(k)], c + 1, n % 2)

            def layer0(c, t):
                at_least(pe, z0_ready, c * T0 + t + 1)
                if t == 0:
                    at_least(pe, x1_ready, c)
                rows = tile_rows(t)
                pe.matmul(acc0[:], w0[0:rows, t, :], z0[0:rows, t % 2, :],
                          start=(t == 0), stop=(t == T0 - 1)).then_inc(l0_step, 1)

            def layer1(c, i, j):
                if j == 0:
                    at_least(pe, z1_ready, c * FI + i + 1)
                    if i == 0:
                        at_least(pe, x2_ready, c)
                mm = pe.matmul(acc1[:], w1[:, i, j, :], z1[:, i % 2, j, :],
                               start=(i == 0 and j == 0), stop=(i == FI - 1 and j == GJ - 1))
                if j == GJ - 1:
                    mm.then_inc(l1_step, 1)

            def turn_x0(c):
                at_least(pe, diag_ready, c * SUBS)
                for s in range(SUBS):
                    last = pe.matmul(x0_t[:, s, :],
                                     x0_parts[:, bass.ds(c * SUBS + s, 1), :, :].rearrange("r o d b -> r (o d b)"),
                                     sel_sum[:], start=True, stop=True)
                last.then_inc(x0t_ready, 1)

            def turn_x2(c):
                at_least(pe, x2_ready, c + 1)
                at_least(pe, x2t_ready, c)
                for s in range(SUBS):
                    last = pe.transpose(x2t_ps[:, s, :], x2[:, s, :], ident[:])
                last.then_inc(x2_turned, 1)

            def sum_products(c, s):
                at_least(pe, diag_ready, c * SUBS + s + 1)
                if s == 0:
                    at_least(pe, x2t_ready, c + 1)
                at_least(pe, g_kept, c * SUBS + max(s - 1, 0))
                pe.matmul(wide[:, s % 2, 0:SB * FG], x2_t[:, s, :],
                          x0_diag[:, s, :, :].rearrange("p b f -> p (b f)"), start=True, stop=True).then_inc(g_ready, 1)

            pe.wait_ge(consts_in, 96)
            pe.wait_ge(dense_in, 16)
            for t in range(GROUPS):
                last = pe.transpose(x0t_ps[0:D, P * t:P * t + P], dense[:, t, :], ident[:])
            last.then_inc(dense_turned, 1)

            turn_parts(0)
            pe.wait_ge(parts_kept, 1)
            pattern(sel_shift[:, T0, :], 0, 1)
            pe.wait_ge(w0_ready, 1)
            for t in range(T0):
                if t == 1:
                    pe.wait_ge(thrice_ready, 1)
                elif t >= 2:
                    pe.wait_ge(z0_ready, t - 1)
                pattern(sel_shift[:, t, 0:tile_rows(t)], 0, t % 2)
                if t >= 1:
                    layer0(0, t - 1)
            layer0(0, T0 - 1)
            pe.wait_ge(z0_ready, T0 - 1)
            pattern(sel_field[:, 0, :], 0, 1)
            pe.wait_ge(w1_in, 16 * FQ)
            pe.wait_ge(w1_pad, 1)
            pe.wait_ge(dense_kept, 1)
            pe.wait_ge(mask_set, 1)

            def body(c, last, groups):
                if not is_first(c):
                    turn_x0(c - 1)
                body_pattern(c, last, ("field", 1))
                for i in range(FI):
                    layer1(c, i, 0)
                    if not last:
                        if i == 0:
                            at_least(pe, parts_kept, groups)
                            body_pattern(c, last, ("thrice", 0))
                        elif 2 * i - 1 < T0:
                            layer0(c + 1, 2 * i - 1)
                    if i == 4 and not is_first(c):
                        turn_x2(c - 1)
                    layer1(c, i, 1)
                    if i > 0 and 2 * i < T0 and not last:
                        body_pattern(c, last, ("shift", 2 * i))
                    if 5 <= i < 5 + SUBS and not is_first(c):
                        sum_products(c - 1, i - 5)
                    layer1(c, i, 2)
                    if not last:
                        if i == 0:
                            body_pattern(c, last, ("shift", 0))
                        elif 2 * i + 1 < T0:
                            body_pattern(c, last, ("shift", 2 * i + 1))
                    layer1(c, i, 3)
                    if i == 0 and not last:
                        body_pattern(c, last, ("shift", 1))
                    if i + 2 <= (FI - 1 if last else FI):
                        body_pattern(c, last, ("field", i + 2))
                    if 2 * i < T0 and not last:
                        layer0(c + 1, 2 * i)

            over_chunks(pe, body, turn_parts)

            turn_x0(CHUNKS - 1)
            turn_x2(CHUNKS - 1)
            for s in range(SUBS):
                sum_products(CHUNKS - 1, s)
            pe.wait_ge(w2_in, 16)
            pe.wait_ge(g_kept, CHUNKS * SUBS)
            for f in range(FIELDS):
                last = pe.matmul(acc1[:], w2[:, f, :], g_sum[:, f, :], start=(f == 0), stop=(f == FIELDS - 1))
            last.then_inc(out2_done, 1)

            pe.wait_ge(top_in, 48)
            pe.wait_ge(out0_ready, CHUNKS)
            for m in range(H1 // P):
                cols = slice(P * m, P * m + P)
                pe.matmul(h1_bank[m], wt1_dense[:, cols], dense_t[:], start=True, stop=False)
                pe.matmul(h1_bank[m], wt1[:, 0, cols], out0[:], start=False, stop=False)
                pe.matmul(h1_bank[m], wt1[:, 1, cols], g_sum[:, FIELDS, :], start=False, stop=False)
            pe.wait_ge(out2_ready, 1)
            for m in range(H1 // P):
                pe.matmul(h1_bank[m], wt1[:, 2, P * m:P * m + P], out2, start=False, stop=True).then_inc(h1_done, 1)
            for k in range(H1 // P):
                pe.wait_ge(h1_ready, k + 1)
                for m in range(H2 // P):
                    mm = pe.matmul(wide[:, m, :], wt2[:, k, P * m:P * m + P], h1[:, k, :],
                                   start=(k == 0), stop=(k == H1 // P - 1))
                    if k == H1 // P - 1:
                        mm.then_inc(h2_done, 1)
            pe.wait_ge(small_in, 48)
            for k in range(H2 // P):
                pe.wait_ge(h2_ready, k + 1)
                last = pe.matmul(y_bank, wt3[:, k:k + 1], h2[:, k, :], start=(k == 0), stop=(k == H2 // P - 1))
            last.then_inc(y_done, 1)


def selectors():
    field = np.zeros((PARTS, FIELDS, FI, P), np.float32)
    for i in range(FI):
        for row in range(P):
            f = FI * (row // GQ) + i
            if f < FIELDS:
                field[:, f, i, row] = 1
    shift = np.zeros((PARTS, FIELDS, T0 + 1, PER_TILE, FIELDS), np.float32)
    for g in range(FIELDS):
        for u in range(PER_TILE):
            shift[:, g, T0, u, g] = 1
            for t in range(T0):
                shift[:, (g + PER_TILE * t + u) % FIELDS, t, u, g] = 1
    total = np.zeros((PARTS, FIELDS, FIELDS), np.float32)
    total[:, np.arange(FIELDS), np.arange(FIELDS)] = 1
    return (field.reshape(PF, FI, P), shift.reshape(PF, T0 + 1, PER_TILE * FIELDS), total.reshape(PF, FIELDS))


def shift_rows():
    upper = np.full((PER_TILE * FIELDS, T0), -1)
    lower = np.full((PER_TILE * FIELDS, T0), -1)
    for s in range(SHIFTS):
        for g in range(FIELDS):
            row, t, h = FIELDS * (s % PER_TILE) + g, s // PER_TILE, (g + s) % FIELDS
            upper[row, t] = g * FIELDS + h
            if s:
                lower[row, t] = h * FIELDS + g
    return upper, lower


def kernel(**inputs):
    import concourse.bacc as bacc
    import ml_dtypes
    from concourse.bass_utils import run_bass_kernel_spmd

    arrays = {name: np.ascontiguousarray(value) for name, value in inputs.items()}
    bf16 = np.dtype(ml_dtypes.bfloat16)
    field, shift, total = selectors()
    arrays["sel_field"], arrays["sel_shift"], arrays["sel_sum"] = field.astype(bf16), shift.astype(bf16), total.astype(bf16)
    arrays["ident"] = np.eye(P, dtype=np.float32)
    arrays["ident_b"] = np.eye(P, dtype=np.float32).astype(bf16)
    arrays["mask"] = np.tile(np.eye(SB, dtype=np.float32), (P // SB, 1))
    w0_rows = arrays.pop("L0_rec_f0")
    for name, rows in zip(("w0_upper", "w0_lower"), shift_rows()):
        laid = np.zeros((*rows.shape, MAPS), w0_rows.dtype)
        laid[rows >= 0] = w0_rows[rows[rows >= 0]]
        arrays[name] = laid

    nc = bacc.Bacc("TRN2", target_bir_lowering=False, num_devices=1)
    a = {name: nc.dram_tensor(f"in_{name}", value.shape, mybir.dt.from_np(value.dtype), kind="ExternalInput").ap()
         for name, value in arrays.items()}
    a["out"] = nc.dram_tensor("out_y", (BATCH, 1), F32, kind="ExternalOutput").ap()
    build_program(nc, a)
    result = run_bass_kernel_spmd(nc, [{f"in_{name}": value for name, value in arrays.items()}], core_ids=[0])
    return result.results[0]["out_y"]
```

```python
from contextlib import ExitStack

import concourse.bass as bass
import numpy as np
from concourse import mybir

F32 = mybir.dt.float32
F32R = mybir.dt.float32r
BF16 = mybir.dt.bfloat16
I32 = mybir.dt.int32
ALU = mybir.AluOpType
ACT = mybir.ActivationFunctionType
AX_X = mybir.AxisListType.X

P = 128
BATCH = 512
FIELDS = 39
D = 16
MAPS = 128
PARTS = 3
PF = PARTS * FIELDS
GROUPS = BATCH // P
CB = 32
CHUNKS = BATCH // CB
PER_GROUP = P // CB
N = CB * D
SHIFTS = (FIELDS + 1) // 2
PER_TILE = 3
T0 = -(-SHIFTS // PER_TILE)
FI, GJ = 10, 4
PAIR, LONE, WHOLE = (0, 1), 2, 3
CUTS = len(PAIR) + 1
FIRST_ORDER = (LONE, *PAIR, WHOLE)
AHEAD = 2
FQ, GQ = P // 32, P // GJ
SB = 8
SUBS = CB // SB
FG = FIELDS + 1
H1, H2 = 512, 256
HALF = BATCH // 2
FIRST_GATHERS = 12
ITEMS0 = T0 + 1 + AHEAD
ITEMS = T0 + 1 + FI


def tile_rows(t):
    return FIELDS * min(PER_TILE, SHIFTS - PER_TILE * t)


def build_program(nc, a):
    w1_rows = a["L0_rec_f1"].rearrange("(f q j) m -> f q (j m)", f=FIELDS, j=GJ)
    w2_rows = a["L0_rec_f2"].rearrange("(f g) m -> g f m", f=FIELDS)
    x1_dram = nc.dram_tensor("x1_dram", [CHUNKS, MAPS, N], F32, kind="Internal").ap()

    with ExitStack() as ctx:
        def sb(name, shape, dt=F32):
            return ctx.enter_context(nc.sbuf_tensor(name, shape, dt))

        def bank(name, shape, dt=F32):
            return ctx.enter_context(nc.psum_tensor(name, shape, dt))

        def sem(name):
            return ctx.enter_context(nc.semaphore(name))

        sel_field = sb("sel_field", [PF, FI, P], BF16)
        sel_shift = sb("sel_shift", [PF, T0 + 1, PER_TILE * FIELDS], BF16)
        sel_sum = sb("sel_sum", [PF, FIELDS], BF16)
        ident_b = sb("ident_b", [P, P], BF16)
        ident = sb("ident", [P, P])
        mask = sb("mask", [P, SB])
        w0 = sb("w0", [PER_TILE * FIELDS, T0, MAPS])
        w1_hi = sb("w1_hi", [P, FI, CUTS, MAPS], F32R)
        w1_lo = sb("w1_lo", [P, FI, CUTS, MAPS], F32R)
        w1_whole = sb("w1_whole", [P, FI, MAPS])
        w2 = sb("w2", [P, FIELDS, MAPS])
        ids = sb("ids_sb", [P, GROUPS, FIELDS], I32)
        ids_now = sb("ids_now", [P, FIELDS], I32)
        emb = sb("emb", [P, FIELDS, D])
        emb_parts = sb("emb_parts", [P, D, PF], BF16)
        x0_parts = sb("x0_parts", [PF, CHUNKS * SUBS, D, SB], BF16)
        x0_thrice = sb("x0_thrice", [PER_TILE * FIELDS, N])
        z0 = sb("z0", [PER_TILE * FIELDS, 2, N])
        x1 = sb("x1", [MAPS, N])
        x1_pat = sb("x1_pat", [P, 2, GJ, N])
        z1 = sb("z1", [P, 2, GJ - 1, N])
        z1_hi = sb("z1_hi", [P, 2, CUTS, N], F32R)
        z1_lo = sb("z1_lo", [P, 2, CUTS, N], F32R)
        x2 = sb("x2", [MAPS, SUBS, D * SB])
        x2_t = sb("x2_t", [P, SUBS, MAPS])
        x0_diag = sb("x0_diag", [P, SUBS, SB, FG])
        g_sum = sb("g_sum", [MAPS, FG, HALF + CB])
        out0 = sb("out0", [MAPS, BATCH])
        out1 = sb("out1", [MAPS, BATCH])
        out2 = sb("out2", [MAPS, BATCH])
        dense = sb("dense_sb", [P, GROUPS, D])
        bias1 = sb("bias1", [P, H1 // P])
        bias2 = sb("bias2", [P, H2 // P])
        wt3 = sb("wt3", [P, H2 // P])
        wt1 = x1_pat[:, 0, 0:3, :]
        wt1_dense = x1_pat[0:D, 0, 3, :]
        wt2 = x1_pat[:, 1, 0:2, :].rearrange("p a (k n) -> p (a k) n", k=2)
        z1_flat = z1[:, :, :, :].rearrange("p a j n -> p (a j) n")
        h1 = z1_flat[:, 0:H1 // P, :]
        h2 = z1_flat[:, H1 // P:H1 // P + H2 // P, :]
        dense_t = x1[0:D, :]
        y = x2[0:1, :, :].rearrange("o s n -> o (s n)")
        g_flat = g_sum[:, :, :].rearrange("g f b -> g (f b)")
        w1_raw = g_flat[:, 0:FI * GJ * MAPS].rearrange("p (f j m) -> p f j m", f=FI, j=GJ)
        w0_mirror = g_flat[0:PER_TILE * FIELDS, FI * GJ * MAPS:FI * GJ * MAPS + T0 * MAPS].rearrange(
            "p (t m) -> p t m", t=T0)

        x1_choice = x2[:, :, :].rearrange("p j (o q) -> p j o q", o=FQ)

        pat = bank("pat", [P, 2, N])
        acc1 = bank("acc1", [MAPS, N])
        acc0 = bank("acc0", [MAPS, N])
        z1_lone = bank("z1_lone", [P, 2, N])
        misc = bank("misc", [P, 2, N])
        turned = misc[:, 0, :]
        sums = misc[:, 1, 0:SB * FG]
        tail_sums = [sums, z1_lone[:, 1, 0:SB * FG]]
        x0_t = turned[:, 0:SUBS * FIELDS].rearrange("p (s f) -> p s f", s=SUBS)
        x2t_ps = turned.rearrange("p (s m) -> p s m", s=SUBS)
        parts_t = misc[:, :, :].bitcast(BF16).rearrange("p a (d b) -> p (a d) b", b=P)
        h1_bank = [pat[:, 0, :], pat[:, 1, :], acc0[:], z1_lone[:, 0, :]]
        h2_bank = [misc[:, 0, :], misc[:, 1, :]]
        x1_first_bank = [acc1[:], misc[:, 0, :], misc[:, 1, :], z1_lone[:, 1, :]]
        y_bank = z1_lone[0:1, 1, :]

        consts_in = sem("consts_in")
        w0_in = sem("w0_in")
        w1_in = sem("w1_in")
        w2_in = sem("w2_in")
        dense_in = sem("dense_in")
        wt1_in = sem("wt1_in")
        wt2_in = sem("wt2_in")
        small_in = sem("small_in")
        ids_in = sem("ids_in")
        ids_staged = sem("ids_staged")
        gathered = sem("gathered")
        split_step = sem("split_step")
        parts_turned = sem("parts_turned")
        parts_kept = sem("parts_kept")
        w0_ready = sem("w0_ready")
        w1_pad = sem("w1_pad")
        w1_hi_ready = sem("w1_hi_ready")
        w1_lo_ready = sem("w1_lo_ready")
        w1_whole_ready = sem("w1_whole_ready")
        mask_set = sem("mask_set")
        dense_turned = sem("dense_turned")
        dense_kept = sem("dense_kept")
        pat_ready = sem("pat_ready")
        thrice_ready = sem("thrice_ready")
        z0_ready = sem("z0_ready")
        l0_step = sem("l0_step")
        x1_ready = sem("x1_ready")
        choice_ready = sem("choice_ready")
        x1_first_made = sem("x1_first_made")
        x1_first_kept = sem("x1_first_kept")
        x1_stored = sem("x1_stored")
        x1_pat_in = sem("x1_pat_in")
        out0_ready = sem("out0_ready")
        z1_ready = sem("z1_ready")
        lone_ready = sem("lone_ready")
        pair_hi_ready = sem("pair_hi_ready")
        pair_lo_ready = sem("pair_lo_ready")
        lone_hi_ready = sem("lone_hi_ready")
        lone_lo_ready = sem("lone_lo_ready")
        whole_step = sem("whole_step")
        pair_high_step = sem("pair_high_step")
        pair_step = sem("pair_step")
        l1_step = sem("l1_step")
        x2_ready = sem("x2_ready")
        x2_turned = sem("x2_turned")
        x2t_ready = sem("x2t_ready")
        x0t_ready = sem("x0t_ready")
        diag_ready = sem("diag_ready")
        g_ready = sem("g_ready")
        g_kept = sem("g_kept")
        out2_done = sem("out2_done")
        out2_ready = sem("out2_ready")
        out1_ready = sem("out1_ready")
        h1_done = sem("h1_done")
        h1_ready = sem("h1_ready")
        h2_done = sem("h2_done")
        h2_ready = sem("h2_ready")
        y_done = sem("y_done")
        y_ready = sem("y_ready")
        y_out = sem("y_out")

        def at_least(eng, s, value):
            if not isinstance(value, int) or value > 0:
                eng.wait_ge(s, value)

        def is_first(c):
            return isinstance(c, int) and c == 0

        def over_chunks(eng, body, halfway):
            body(0, False, 1, 0, None)
            body(1, False, 1, 0, None)
            with eng.Fori(0, GROUPS - 2) as t:
                body(t * PER_GROUP + 2, False, t + 1, 0, t + 1)
                with eng.Fori(1, PER_GROUP) as q:
                    body(t * PER_GROUP + q + 2, False, t + 2, 0, None)
            halfway()
            body(CHUNKS - PER_GROUP - 2, False, GROUPS - 1, -HALF, GROUPS - 1)
            with eng.Fori(CHUNKS - PER_GROUP - 1, CHUNKS - 2) as c:
                body(c, False, GROUPS, -HALF, None)
            body(CHUNKS - 2, False, GROUPS, -HALF, None)
            body(CHUNKS - 1, True, GROUPS, -HALF, None)

        def shifts(i):
            return [0] if i == 0 else [t for t in (2 * i - 1, 2 * i) if t < T0]

        def order(last):
            fields = [("field", i + AHEAD) for i in range(FI - AHEAD if last else FI)]
            if last:
                return fields
            found = []
            for i, field in enumerate(fields):
                found.append(field)
                if i == 0:
                    found.append(("thrice", 0))
                found += [("shift", t) for t in shifts(i)]
            return found

        def pattern_ready(eng, c, last, what):
            n = order(last).index(what)
            at_least(eng, pat_ready, c * ITEMS + ITEMS0 + n + 1)
            return n % 2

        block = ctx.enter_context(nc.Block())

        @block.sync
        def _(sp):
            sp.dma_start(ids[:], a["ids"].rearrange("(t p) f -> p t f", p=P)).then_inc(ids_in, 16)
            for dst, name in ((ident_b, "ident_b"), (sel_shift, "sel_shift"), (sel_field, "sel_field"),
                              (sel_sum, "sel_sum"), (ident, "ident"), (mask, "mask")):
                sp.dma_start(dst[:], a[name]).then_inc(consts_in, 16)
            sp.dma_start(w0[:], a["w0_upper"]).then_inc(w0_in, 16)
            sp.dma_start(w0_mirror, a["w0_lower"]).then_inc(w0_in, 16)
            sp.dma_start(dense[:], a["dense_ctx"].rearrange("(t p) d -> p t d", p=P)).then_inc(dense_in, 16)
            for fq in range(FQ):
                fields = min(FI, FIELDS - FI * fq)
                sp.dma_start(w1_raw[32 * fq:32 * fq + 32, 0:fields, :, :].rearrange("p f j m -> p f (j m)"),
                             w1_rows[FI * fq:FI * fq + fields, :, :].rearrange("f q n -> q f n")).then_inc(w1_in, 16)
            sp.dma_start(w2[:], w2_rows).then_inc(w2_in, 16)
            with nc.allow_non_contiguous_dma(reason="a few hundred words"):
                sp.dma_start(bias1[:], a["b_top1"].rearrange("(k p) -> p k", p=P)).then_inc(small_in, 16)
                sp.dma_start(bias2[:], a["b_top2"].rearrange("(k p) -> p k", p=P)).then_inc(small_in, 16)
                sp.dma_start(wt3[:], a["W_top3"].rearrange("(k p) o -> p (k o)", p=P)).then_inc(small_in, 16)

            def spread(c):
                at_least(sp, x1_ready, c + 1)
                sp.dma_start(x1_dram[c], x1[:]).then_inc(x1_stored, 16)
                at_least(sp, x1_stored, 16 * c)
                if not (isinstance(c, int) and c == 1):
                    at_least(sp, z1_ready, FI * c - FI)
                for fq in range(FQ):
                    sp.dma_start(x1_pat[32 * fq:32 * fq + 32, c % 2, :, :].rearrange("q j n -> q (j n)"),
                                 x1_dram[c].rearrange("(q j) n -> q (j n)", j=GJ)).then_inc(x1_pat_in, 16)

            spread(1)
            with sp.Fori(2, CHUNKS) as c:
                spread(c)
            sp.wait_ge(z1_ready, FI * (CHUNKS - 1))
            sp.dma_start(wt1, a["W_top1"][0:3 * MAPS, :].rearrange("(k p) n -> p k n", p=P)).then_inc(wt1_in, 16)
            sp.dma_start(wt1_dense, a["W_top1"][3 * MAPS:3 * MAPS + D, :]).then_inc(wt1_in, 16)
            sp.wait_ge(z1_ready, FI * CHUNKS)
            sp.dma_start(wt2, a["W_top2"].rearrange("(k p) n -> p k n", p=P)).then_inc(wt2_in, 16)
            sp.wait_ge(y_ready, 1)
            sp.dma_start(a["out"].rearrange("b o -> o b"), y).then_inc(y_out, 16)
            sp.wait_ge(y_out, 16)

        @block.gpsimd
        def _(pool):
            def stage_ids(t):
                if not is_first(t):
                    pool.wait_ge(gathered, t * (16 * FIELDS))
                pool.tensor_copy(ids_now[:], ids[:, bass.ds(t, 1), :].rearrange("p o f -> p (o f)")).then_inc(ids_staged, 1)
                at_least(pool, ids_staged, t + 1)
                at_least(pool, split_step, t * 4)

            def gather(fields):
                for f in fields:
                    pool.indirect_dma_start(
                        out=emb[:, f, :], out_offset=None, in_=a[f"tbl_{f}"][:, :],
                        in_offset=bass.IndirectOffsetOnAxis(ap=ids_now[:, f:f + 1], axis=0),
                    ).then_inc(gathered, 16)

            def cut_pair(c, i):
                at_least(pool, pair_hi_ready, c * FI + i + 1)
                if not (is_first(c) and i < 2):
                    at_least(pool, pair_step, c * FI + (i - 1))
                pool.tensor_tensor(z1_lo[:, i % 2, 0:2, :], z1[:, i % 2, 0:2, :],
                                   z1_hi[:, i % 2, 0:2, :].bitcast(F32), ALU.subtract).then_inc(pair_lo_ready, 1)

            def body(c, last, fields):
                for i in range(FI):
                    if i + AHEAD < FI:
                        cut_pair(c, i + AHEAD)
                    elif not last:
                        cut_pair(c + 1, i + AHEAD - FI)
                    share = 3 if i < 4 else 1
                    gather(fields[:share])
                    fields = fields[share:]

            def part_of(fields, q, n):
                size = -(-len(fields) // n)
                return fields[size * q:size * q + size]

            pool.wait_ge(ids_in, 16)
            stage_ids(0)
            gather(range(FIELDS))
            pool.wait_ge(w1_hi_ready, 1)
            pool.tensor_tensor(w1_lo[:], w1_raw[:, :, 0:CUTS, :], w1_hi[:].bitcast(F32),
                               ALU.subtract).then_inc(w1_lo_ready, 1)
            stage_ids(1)
            gather(range(FIRST_GATHERS))
            for i in range(AHEAD):
                cut_pair(0, i)
            for c in range(2):
                body(c, False, part_of(range(FIRST_GATHERS, FIELDS), c, 2))
            with pool.Fori(0, GROUPS - 2) as t:
                body(t * PER_GROUP + 2, False, [])
                stage_ids(t + 2)
                for q in range(1, PER_GROUP):
                    body(t * PER_GROUP + q + 2, False, part_of(range(FIELDS), q - 1, PER_GROUP - 1))
            with pool.Fori(CHUNKS - PER_GROUP - 2, CHUNKS - 2) as c:
                body(c, False, [])
            body(CHUNKS - 2, False, [])
            body(CHUNKS - 1, True, [])

        @block.vector
        def _(dve):
            def cut_embeddings(t, k):
                value = emb[:, :, :].rearrange("p f d -> p d f")
                part = [emb_parts[:, :, FIELDS * j:FIELDS * j + FIELDS] for j in range(PARTS)]
                if k == 0:
                    at_least(dve, gathered, t * (16 * FIELDS) + 16 * FIELDS)
                    at_least(dve, parts_turned, t)
                    dve.tensor_copy(part[0], value).then_inc(split_step, 1)
                elif k == 1:
                    at_least(dve, split_step, t * 4 + 1)
                    dve.tensor_tensor(value, value, part[0], ALU.subtract).then_inc(split_step, 1)
                elif k == 2:
                    at_least(dve, split_step, t * 4 + 2)
                    dve.tensor_copy(part[1], value).then_inc(split_step, 1)
                else:
                    at_least(dve, split_step, t * 4 + 3)
                    dve.tensor_tensor(part[2], value, part[1], ALU.subtract).then_inc(split_step, 1)

            dve.memset(w1_raw[32 * (FQ - 1):P, FI - 1, :, :], 0.0).then_inc(w1_pad, 1)
            dve.wait_ge(consts_in, 96)
            dve.tensor_copy(x0_diag[:, :, :, FIELDS], mask[:].rearrange("p (o b) -> p o b", o=1)
                            .to_broadcast([P, SUBS, SB])).then_inc(mask_set, 1)
            for j in range(GJ):
                dve.tensor_copy(x1_choice[:, j, :, :], ident[:].rearrange("p (o q j) -> p j o q", o=1, j=GJ)[:, j, :, :]
                                .to_broadcast([P, FQ, GQ])).then_inc(choice_ready, 1)
            dve.wait_ge(w0_in, 32)
            dve.tensor_tensor(w0[:], w0[:], w0_mirror, ALU.add).then_inc(w0_ready, 1)
            for k in range(4):
                cut_embeddings(0, k)

            def products0(c, t, bank_of):
                rows = tile_rows(t)
                if t == 0:
                    at_least(dve, thrice_ready, c + 1)
                if not (isinstance(c, int) and c == 0 and t < 2):
                    at_least(dve, l0_step, c * T0 + max(t - 1, 0))
                dve.tensor_tensor(z0[0:rows, t % 2, :], pat[0:rows, bank_of, :], x0_thrice[0:rows, :],
                                  ALU.mult).then_inc(z0_ready, 1)

            def products1(c, i, bank_of):
                early = is_first(c) and i < 2
                first = i == 0 and is_first(c)
                if first:
                    dve.wait_ge(x1_first_kept, 1)
                elif i == 0:
                    at_least(dve, x1_pat_in, c * (16 * FQ))
                if not early:
                    at_least(dve, lone_lo_ready, c * FI + (i - 1))
                dve.tensor_tensor(z1_lone[:, i % 2, :], pat[:, bank_of, :], x1_pat[:, c % 2, LONE, :],
                                  ALU.mult).then_inc(lone_ready, 1)
                if not early:
                    at_least(dve, pair_lo_ready, c * FI + (i - 1))
                    at_least(dve, whole_step, c * FI + (i - 1))
                if first:
                    dve.wait_ge(x1_first_kept, 1 + len(PAIR))
                dve.tensor_tensor(z1[:, i % 2, 0:2, :], pat[:, bank_of:bank_of + 1, :].to_broadcast([P, 2, N]),
                                  x1_pat[:, c % 2, 0:2, :], ALU.mult)
                if first:
                    dve.wait_ge(x1_first_kept, GJ)
                dve.tensor_tensor(z1[:, i % 2, 2, :], pat[:, bank_of, :], x1_pat[:, c % 2, WHOLE, :],
                                  ALU.mult).then_inc(z1_ready, 1)

            def cut_lone(c, i):
                at_least(dve, lone_hi_ready, c * FI + i + 1)
                if not (is_first(c) and i < 2):
                    at_least(dve, l1_step, c * FI + (i - 1))
                dve.tensor_tensor(z1_lo[:, i % 2, LONE, :], z1_lone[:, i % 2, :],
                                  z1_hi[:, i % 2, LONE, :].bitcast(F32), ALU.subtract).then_inc(lone_lo_ready, 1)

            def sum_x1(c):
                at_least(dve, x1_ready, c + 1)
                dve.tensor_reduce(out0[:, bass.ds(c * CB, CB)].rearrange("m (s b) -> m s b", s=SUBS),
                                  x1[:].rearrange("m (s d b) -> m s b d", s=SUBS, d=D),
                                  AX_X, ALU.add).then_inc(out0_ready, 1)

            def diagonal(c, s):
                if s == 0:
                    at_least(dve, x0t_ready, c + 1)
                    at_least(dve, g_ready, c * SUBS)
                dve.tensor_tensor(
                    x0_diag[:, s, :, 0:FIELDS], x0_t[:, s:s + 1, :].to_broadcast([P, SB, FIELDS]),
                    mask[:].rearrange("p (b o) -> p b o", o=1).to_broadcast([P, SB, FIELDS]),
                    ALU.mult).then_inc(diag_ready, 1)

            for t in range(T0):
                dve.wait_ge(pat_ready, t + 2)
                products0(0, t, (t + 1) % 2)
            for i in range(AHEAD):
                dve.wait_ge(pat_ready, T0 + 2 + i)
                products1(0, i, (T0 + 1 + i) % 2)
            sum_x1(0)
            cut_lone(0, 0)

            def body(c, last, groups, place, group):
                for i in range(FI):
                    if not is_first(c):
                        for s in range(SUBS) if i == 4 else []:
                            diagonal(c - 1, s)
                    if i + AHEAD < FI:
                        products1(c, i + AHEAD, pattern_ready(dve, c, last, ("field", i + AHEAD)))
                    elif not last:
                        products1(c + 1, i + AHEAD - FI, pattern_ready(dve, c, last, ("field", i + AHEAD)))
                    if i + 1 < FI:
                        cut_lone(c, i + 1)
                    elif not last:
                        cut_lone(c + 1, 0)
                    if not last:
                        for t in shifts(i):
                            products0(c + 1, t, pattern_ready(dve, c, last, ("shift", t)))
                    if group is not None and 1 <= i < 5:
                        cut_embeddings(group, i - 1)
                    if i == 6 and not last:
                        sum_x1(c + 1)

            over_chunks(dve, body, lambda: None)
            for s in range(SUBS):
                diagonal(CHUNKS - 1, s)
            dve.wait_ge(dense_turned, 1)
            dve.wait_ge(x1_stored, 16 * (CHUNKS - 1))
            dve.wait_ge(out0_ready, CHUNKS)
            dve.tensor_copy(dense_t, pat[0:D, 0, :]).then_inc(dense_kept, 1)

        @block.scalar
        def _(act):
            def keep_parts(t):
                at_least(act, parts_turned, t + 1)
                act.copy(x0_parts[:, bass.ds(t * (PER_GROUP * SUBS), PER_GROUP * SUBS), :, :],
                         parts_t[0:PF, :, :].rearrange("r d (s b) -> r s d b", b=SB)).then_inc(parts_kept, 1)

            def keep_thrice(c, bank_of):
                at_least(act, z0_ready, c * T0)
                act.copy(x0_thrice[:], pat[0:PER_TILE * FIELDS, bank_of, :]).then_inc(thrice_ready, 1)

            def keep_x1(c):
                at_least(act, l0_step, c * T0 + T0)
                at_least(act, x1_stored, c * 16 - 16)
                at_least(act, out0_ready, c)
                act.copy(x1[:], acc0[:]).then_inc(x1_ready, 1)

            def keep_x2(c):
                at_least(act, l1_step, c * FI + FI)
                at_least(act, x2_turned, c)
                act.copy(x2[:], acc1[:].rearrange("m (s n) -> m s n", s=SUBS)).then_inc(x2_ready, 1)

            def keep_x2_t(c):
                at_least(act, x2_turned, c + 1)
                at_least(act, g_ready, c * SUBS)
                act.copy(x2_t[:], x2t_ps).then_inc(x2t_ready, 1)

            def keep_g(c, s, place, bank_of=sums):
                at_least(act, g_ready, c * SUBS + s + 1)
                act.copy(g_sum[:, :, bass.ds(c * CB + (s * SB + place), SB)],
                         bank_of.rearrange("g (b f) -> g f b", b=SB)).then_inc(g_kept, 1)

            def high_pair(c, i):
                at_least(act, z1_ready, c * FI + i + 1)
                if not (is_first(c) and i < 2):
                    at_least(act, pair_high_step, c * FI + (i - 1))
                    at_least(act, pair_lo_ready, c * FI + (i - 1))
                act.copy(z1_hi[:, i % 2, 0:2, :], z1[:, i % 2, 0:2, :]).then_inc(pair_hi_ready, 1)

            def high_lone(c, i):
                at_least(act, lone_ready, c * FI + i + 1)
                if not (is_first(c) and i < 2):
                    at_least(act, l1_step, c * FI + (i - 1))
                act.copy(z1_hi[:, i % 2, LONE, :], z1_lone[:, i % 2, :]).then_inc(lone_hi_ready, 1)

            act.wait_ge(w1_in, 16 * FQ)
            act.wait_ge(w1_pad, 1)
            act.copy(w1_hi[:], w1_raw[:, :, 0:CUTS, :]).then_inc(w1_hi_ready, 1)
            act.copy(w1_whole[:], w1_raw[:, :, WHOLE, :]).then_inc(w1_whole_ready, 1)
            keep_parts(0)
            act.wait_ge(pat_ready, 1)
            keep_thrice(0, 0)
            keep_x1(0)
            for n, j in enumerate(FIRST_ORDER):
                act.wait_ge(x1_first_made, n + 1)
                act.copy(x1_pat[:, 0, j, :], x1_first_bank[n]).then_inc(x1_first_kept, 1)
            high_lone(0, 0)
            for i in range(AHEAD):
                high_pair(0, i)

            def body(c, last, groups, place, group):
                for i in range(FI):
                    if i == 0 and not last:
                        keep_thrice(c + 1, pattern_ready(act, c, last, ("thrice", 0)))
                    if i + 1 < FI:
                        high_lone(c, i + 1)
                    elif not last:
                        high_lone(c + 1, 0)
                    if i == FI - 1:
                        keep_x2(c)
                    if i + AHEAD < FI:
                        high_pair(c, i + AHEAD)
                    elif not last:
                        high_pair(c + 1, i + AHEAD - FI)
                    if i == 4 and not is_first(c):
                        keep_x2_t(c - 1)
                    if i == 4 and not last:
                        keep_x1(c + 1)
                    if i == 5 and group is not None:
                        keep_parts(group)
                    if i - 6 in range(SUBS) and not is_first(c):
                        keep_g(c - 1, i - 6, place)

            def halfway():
                act.copy(out1[:, 0:HALF], g_sum[:, FIELDS, 0:HALF]).then_inc(out1_ready, 1)
                act.wait_ge(out1_ready, 1)
                act.wait_ge(out2_done, 1)
                act.copy(out2[:, 0:HALF], acc0[:, 0:HALF]).then_inc(out2_ready, 1)

            over_chunks(act, body, halfway)
            keep_x2_t(CHUNKS - 1)
            for s in range(SUBS):
                keep_g(CHUNKS - 1, s, -HALF, tail_sums[s % 2])
            act.wait_ge(g_kept, CHUNKS * SUBS)
            act.copy(out1[:, HALF + CB:BATCH], g_sum[:, FIELDS, CB:HALF]).then_inc(out1_ready, 1)
            act.copy(out1[:, HALF:HALF + CB], g_sum[:, FIELDS, HALF:HALF + CB]).then_inc(out1_ready, 1)
            act.wait_ge(out2_done, 2)
            act.copy(out2[:, HALF + CB:BATCH], acc1[:, 0:HALF - CB]).then_inc(out2_ready, 1)
            act.copy(out2[:, HALF:HALF + CB], acc1[:, HALF - CB:HALF]).then_inc(out2_ready, 1)
            act.wait_ge(small_in, 48)
            for m in range(H1 // P):
                act.wait_ge(h1_done, m + 1)
                act.activation(h1[:, m, :], h1_bank[m], ACT.Relu, bias=bias1[:, m:m + 1]).then_inc(h1_ready, 1)
            for m in range(H2 // P):
                act.wait_ge(h2_done, m + 1)
                act.activation(h2[:, m, :], h2_bank[m], ACT.Relu, bias=bias2[:, m:m + 1]).then_inc(h2_ready, 1)
            act.wait_ge(y_done, 1)
            act.copy(y, y_bank).then_inc(y_ready, 1)

        @block.tensor
        def _(pe):
            def turn_parts(t):
                at_least(pe, split_step, t * 4 + 4)
                if not is_first(t):
                    at_least(pe, g_kept, t * (PER_GROUP * SUBS) - (PER_GROUP - 1) * SUBS)
                    at_least(pe, x2t_ready, t * PER_GROUP - (PER_GROUP - 2))
                for d in range(D):
                    last = pe.transpose(parts_t[0:PF, d, :], emb_parts[:, d, :], ident_b[:])
                last.then_inc(parts_turned, 1)

            def parts(c):
                return x0_parts[:, bass.ds(c * SUBS, SUBS), :, :].rearrange("r s d b -> r (s d b)")

            def pattern(sel, c, bank_of):
                pe.matmul(pat[0:sel.shape[1], bank_of, :], sel, parts(c), start=True, stop=True).then_inc(pat_ready, 1)

            def body_pattern(c, last, what):
                n = order(last).index(what)
                if n >= 2:
                    before, k = order(last)[n - 2]
                    if before == "field":
                        at_least(pe, z1_ready, c * FI + k + 1)
                    elif before == "thrice":
                        at_least(pe, thrice_ready, c + 2)
                    else:
                        at_least(pe, z0_ready, c * T0 + (T0 + k + 1))
                else:
                    at_least(pe, z1_ready, c * FI + n + 1)
                kind, k = what
                if kind == "field":
                    pattern(sel_field[:, k % FI, :], c + k // FI, n % 2)
                elif kind == "thrice":
                    pattern(sel_shift[:, T0, :], c + 1, n % 2)
                else:
                    pattern(sel_shift[:, k, 0:tile_rows(k)], c + 1, n % 2)

            def layer0(c, t, halves=0):
                at_least(pe, z0_ready, c * T0 + t + 1)
                if t == 0:
                    at_least(pe, x1_ready, c)
                    if halves:
                        at_least(pe, out2_ready, halves)
                rows = tile_rows(t)
                pe.matmul(acc0[:], w0[0:rows, t, :], z0[0:rows, t % 2, :],
                          start=(t == 0), stop=(t == T0 - 1)).then_inc(l0_step, 1)

            def layer1_whole(c, i):
                at_least(pe, z1_ready, c * FI + i + 1)
                if i == 0:
                    at_least(pe, x2_ready, c)
                pe.matmul(acc1[:], w1_whole[:, i, :], z1[:, i % 2, 2, :],
                          start=(i == 0), stop=False).then_inc(whole_step, 1)

            def layer1_high(i, j):
                pe.matmul(acc1[:], w1_hi[:, i, j, :], z1_hi[:, i % 2, j, :], start=False, stop=False)
                return pe.matmul(acc1[:], w1_lo[:, i, j, :], z1_hi[:, i % 2, j, :], start=False, stop=False)

            def layer1_low(i, j, stop=False):
                return pe.matmul(acc1[:], w1_hi[:, i, j, :], z1_lo[:, i % 2, j, :], start=False, stop=stop)

            def layer1_pair_high(c, i, j):
                if j == PAIR[0]:
                    at_least(pe, pair_hi_ready, c * FI + i + 1)
                last = layer1_high(i, j)
                if j == PAIR[-1]:
                    last.then_inc(pair_high_step, 1)

            def layer1_pair_low(c, i):
                at_least(pe, pair_lo_ready, c * FI + i + 1)
                for j in PAIR:
                    last = layer1_low(i, j)
                last.then_inc(pair_step, 1)

            def layer1_lone(c, i):
                at_least(pe, lone_hi_ready, c * FI + i + 1)
                layer1_high(i, LONE)
                at_least(pe, lone_lo_ready, c * FI + i + 1)
                layer1_low(i, LONE, stop=(i == FI - 1)).then_inc(l1_step, 1)

            def turn_x0(c):
                at_least(pe, x2t_ready, c)
                for s in range(SUBS):
                    last = pe.matmul(x0_t[:, s, :],
                                     x0_parts[:, bass.ds(c * SUBS + s, 1), :, :].rearrange("r o d b -> r (o d b)"),
                                     sel_sum[:], start=True, stop=True)
                last.then_inc(x0t_ready, 1)

            def turn_x2(c):
                at_least(pe, x2_ready, c + 1)
                at_least(pe, diag_ready, c * SUBS + SUBS)
                for s in range(SUBS):
                    last = pe.transpose(x2t_ps[:, s, :], x2[:, s, :], ident[:])
                last.then_inc(x2_turned, 1)

            def sum_products(c, s, kept, into):
                if s == 0:
                    at_least(pe, x2t_ready, c + 1)
                at_least(pe, g_kept, kept)
                pe.matmul(into, x2_t[:, s, :],
                          x0_diag[:, s, :, :].rearrange("p b f -> p (b f)"), start=True, stop=True).then_inc(g_ready, 1)

            def layer2(acc, first):
                for f in range(FIELDS):
                    last = pe.matmul(acc[:, 0:HALF], w2[:, f, :], g_sum[:, f, first:first + HALF],
                                     start=(f == 0), stop=(f == FIELDS - 1))
                last.then_inc(out2_done, 1)

            pe.wait_ge(consts_in, 96)
            pe.wait_ge(mask_set, 1)

            turn_parts(0)
            pe.wait_ge(parts_kept, 1)
            pattern(sel_shift[:, T0, :], 0, 0)
            pe.wait_ge(w0_ready, 1)
            for t in range(T0):
                if t == 1:
                    pe.wait_ge(thrice_ready, 1)
                elif t >= 2:
                    pe.wait_ge(z0_ready, t - 1)
                pattern(sel_shift[:, t, 0:tile_rows(t)], 0, (t + 1) % 2)
                if t >= 1:
                    layer0(0, t - 1)
            for i in range(AHEAD):
                pe.wait_ge(z0_ready, T0 - 1 + i)
                if i == 0:
                    pattern(sel_field[:, i, :], 0, (T0 + 1 + i) % 2)
                    layer0(0, T0 - 1)
                else:
                    pattern(sel_field[:, i, :], 0, (T0 + 1 + i) % 2)
            pe.wait_ge(choice_ready, GJ)
            pe.wait_ge(x1_ready, 1)
            for n, j in enumerate(FIRST_ORDER):
                pe.matmul(x1_first_bank[n], x1_choice[:, j, :, :].rearrange("p o q -> p (o q)"), x1[:], start=True, stop=True).then_inc(x1_first_made, 1)
            pe.wait_ge(w1_whole_ready, 1)
            pe.wait_ge(w1_hi_ready, 1)
            pe.wait_ge(w1_lo_ready, 1)

            def body(c, last, groups, place, group):
                for i in range(FI):
                    if i + AHEAD < FI or not last:
                        body_pattern(c, last, ("field", i + AHEAD))
                    if i == 0:
                        at_least(pe, parts_kept, groups)
                        if not last:
                            body_pattern(c, last, ("thrice", 0))
                        if not is_first(c):
                            turn_x0(c - 1)
                    layer1_whole(c, i)
                    now = [] if last else shifts(i)
                    before = [] if last or i == 0 else shifts(i - 1)
                    for t in before:
                        layer0(c + 1, t, halves=1 if place else 0)
                    layer1_pair_high(c, i, PAIR[0])
                    if len(now) == 2:
                        body_pattern(c, last, ("shift", now[0]))
                    layer1_pair_high(c, i, PAIR[1])
                    layer1_pair_low(c, i)
                    if i == 5 and group is not None:
                        turn_parts(group)
                    if len(now) == 2:
                        body_pattern(c, last, ("shift", now[1]))
                    layer1_lone(c, i)
                    if len(now) == 1:
                        body_pattern(c, last, ("shift", now[0]))
                    if i == 4 and not is_first(c):
                        turn_x2(c - 1)
                    if i - 6 in range(SUBS) and not is_first(c):
                        if i == 6 and group is not None:
                            at_least(pe, parts_kept, group + 1)
                        sum_products(c - 1, i - 6, (c - 1) * SUBS + (i - 6), sums)

            def halfway():
                pe.wait_ge(w2_in, 16)
                pe.wait_ge(g_kept, CHUNKS // 2 * SUBS)
                layer2(acc0, 0)

            over_chunks(pe, body, halfway)

            turn_x0(CHUNKS - 1)
            pe.wait_ge(dense_in, 16)
            for t in range(GROUPS):
                last = pe.transpose(pat[0:D, 0, P * t:P * t + P], dense[:, t, :], ident[:])
            last.then_inc(dense_turned, 1)
            pe.wait_ge(wt1_in, 32)
            pe.wait_ge(out0_ready, CHUNKS)

            def top1_out0(m):
                pe.matmul(h1_bank[m], wt1[:, 0, P * m:P * m + P], out0[:], start=True, stop=False)

            def top1_dense(m):
                pe.matmul(h1_bank[m], wt1_dense[:, P * m:P * m + P], dense_t, start=False, stop=False)

            for m in range(1, H1 // P):
                top1_out0(m)
            turn_x2(CHUNKS - 1)
            pe.wait_ge(dense_kept, 1)
            top1_dense(1)
            top1_dense(2)
            before = (CHUNKS - 1) * SUBS
            sum_products(CHUNKS - 1, 0, before, tail_sums[0])
            sum_products(CHUNKS - 1, 1, before, tail_sums[1])
            top1_out0(0)
            sum_products(CHUNKS - 1, 2, before + 1, tail_sums[0])
            top1_dense(0)
            sum_products(CHUNKS - 1, 3, before + 2, tail_sums[1])
            top1_dense(3)
            pe.wait_ge(g_kept, CHUNKS * SUBS)
            layer2(acc1, CB)

            pe.wait_ge(out1_ready, 3)
            for m in range(H1 // P):
                pe.matmul(h1_bank[m], wt1[:, 1, P * m:P * m + P], out1[:], start=False, stop=False)
            pe.wait_ge(out2_ready, 3)
            for m in range(H1 // P):
                pe.matmul(h1_bank[m], wt1[:, 2, P * m:P * m + P], out2[:], start=False, stop=True).then_inc(h1_done, 1)
            pe.wait_ge(wt2_in, 16)
            for k in range(H1 // P):
                pe.wait_ge(h1_ready, k + 1)
                for m in range(H2 // P):
                    mm = pe.matmul(h2_bank[m], wt2[:, k, P * m:P * m + P], h1[:, k, :],
                                   start=(k == 0), stop=(k == H1 // P - 1))
                    if k == H1 // P - 1:
                        mm.then_inc(h2_done, 1)
            pe.wait_ge(small_in, 48)
            for k in range(H2 // P):
                pe.wait_ge(h2_ready, k + 1)
                last = pe.matmul(y_bank, wt3[:, k:k + 1], h2[:, k, :], start=(k == 0), stop=(k == H2 // P - 1))
            last.then_inc(y_done, 1)


def selectors():
    field = np.zeros((PARTS, FIELDS, FI, P), np.float32)
    for i in range(FI):
        for row in range(P):
            f = FI * (row // GQ) + i
            if f < FIELDS:
                field[:, f, i, row] = 1
    shift = np.zeros((PARTS, FIELDS, T0 + 1, PER_TILE, FIELDS), np.float32)
    for g in range(FIELDS):
        for u in range(PER_TILE):
            shift[:, g, T0, u, g] = 1
            for t in range(T0):
                shift[:, (g + PER_TILE * t + u) % FIELDS, t, u, g] = 1
    total = np.zeros((PARTS, FIELDS, FIELDS), np.float32)
    total[:, np.arange(FIELDS), np.arange(FIELDS)] = 1
    return (field.reshape(PF, FI, P), shift.reshape(PF, T0 + 1, PER_TILE * FIELDS), total.reshape(PF, FIELDS))


def shift_rows():
    upper = np.full((PER_TILE * FIELDS, T0), -1)
    lower = np.full((PER_TILE * FIELDS, T0), -1)
    for s in range(SHIFTS):
        for g in range(FIELDS):
            row, t, h = FIELDS * (s % PER_TILE) + g, s // PER_TILE, (g + s) % FIELDS
            upper[row, t] = g * FIELDS + h
            if s:
                lower[row, t] = h * FIELDS + g
    return upper, lower


def kernel(**inputs):
    import concourse.bacc as bacc
    import ml_dtypes
    from concourse.bass_utils import run_bass_kernel_spmd

    arrays = {name: np.ascontiguousarray(value) for name, value in inputs.items()}
    bf16 = np.dtype(ml_dtypes.bfloat16)
    field, shift, total = selectors()
    arrays["sel_field"], arrays["sel_shift"], arrays["sel_sum"] = field.astype(bf16), shift.astype(bf16), total.astype(bf16)
    arrays["ident"] = np.eye(P, dtype=np.float32)
    arrays["ident_b"] = np.eye(P, dtype=np.float32).astype(bf16)
    arrays["mask"] = np.tile(np.eye(SB, dtype=np.float32), (P // SB, 1))
    w0_rows = arrays.pop("L0_rec_f0")
    for name, rows in zip(("w0_upper", "w0_lower"), shift_rows()):
        laid = np.zeros((*rows.shape, MAPS), w0_rows.dtype)
        laid[rows >= 0] = w0_rows[rows[rows >= 0]]
        arrays[name] = laid

    nc = bacc.Bacc("TRN2", target_bir_lowering=False, num_devices=1)
    a = {name: nc.dram_tensor(f"in_{name}", value.shape, mybir.dt.from_np(value.dtype), kind="ExternalInput").ap()
         for name, value in arrays.items()}
    a["out"] = nc.dram_tensor("out_y", (BATCH, 1), F32, kind="ExternalOutput").ap()
    build_program(nc, a)
    result = run_bass_kernel_spmd(nc, [{f"in_{name}": value for name, value in arrays.items()}], core_ids=[0])
    return result.results[0]["out_y"]
```

```python
from contextlib import ExitStack

import concourse.bass as bass
import numpy as np
from concourse import mybir

F32 = mybir.dt.float32
F32R = mybir.dt.float32r
BF16 = mybir.dt.bfloat16
I32 = mybir.dt.int32
ALU = mybir.AluOpType
ACT = mybir.ActivationFunctionType
AX_X = mybir.AxisListType.X

P = 128
BATCH = 512
FIELDS = 39
D = 16
MAPS = 128
PARTS = 3
PF = PARTS * FIELDS
GROUPS = BATCH // P
CB = 32
CHUNKS = BATCH // CB
PER_GROUP = P // CB
N = CB * D
SHIFTS = (FIELDS + 1) // 2
PER_TILE = 3
T0 = -(-SHIFTS // PER_TILE)
FI, GJ = 10, 4
LONE, PAIR, WHOLE = 0, (1, 2), 3
CUTS = len(PAIR) + 1
AHEAD = 2
FQ, GQ = P // 32, P // GJ
SB = 8
SUBS = CB // SB
FG = FIELDS + 1
H1, H2 = 512, 256
HALF = BATCH // 2
FIRST_GATHERS = 12
ITEMS0 = T0 + 1 + AHEAD
ITEMS = T0 + 1 + FI


SMALL_ROWS = 10 * P
SMALL_TABLES = 14
ONE_HOTS = 6


def fold(rows):
    parts = max(n for n in range(1, P + 1) if rows % n == 0)
    return parts, rows // parts


def runs(fields):
    found = []
    for n, f in enumerate(fields):
        if found and found[-1][1] + found[-1][2] == f:
            found[-1] = (*found[-1][:2], found[-1][2] + 1)
        else:
            found.append((n, f, 1))
    return found


def tile_rows(t):
    return FIELDS * min(PER_TILE, SHIFTS - PER_TILE * t)


def build_program(nc, a):
    w1_rows = a["L0_rec_f1"].rearrange("(f q j) m -> f q (j m)", f=FIELDS, j=GJ)
    w2_rows = a["L0_rec_f2"].rearrange("(f g) m -> g f m", f=FIELDS)
    small = [f for f in range(FIELDS) if fold(a[f"tbl_{f}"].shape[0])[1] <= SMALL_ROWS // P][:SMALL_TABLES]
    large = [f for f in range(FIELDS) if f not in small]
    folds = [fold(a[f"tbl_{f}"].shape[0]) for f in small]
    assert len({used for used, _ in folds}) == 1
    small_used = folds[0][0]
    first_row = [sum(k for _, k in folds[:n]) for n in range(len(small) + 1)]
    half_of = [0, len(small) // 2, len(small)]
    small_halves = [range(half_of[h], half_of[h + 1]) for h in range(2)]
    x1_dram = nc.dram_tensor("x1_dram", [CHUNKS, MAPS, N], F32, kind="Internal").ap()

    with ExitStack() as ctx:
        def sb(name, shape, dt=F32):
            return ctx.enter_context(nc.sbuf_tensor(name, shape, dt))

        def bank(name, shape, dt=F32):
            return ctx.enter_context(nc.psum_tensor(name, shape, dt))

        def sem(name):
            return ctx.enter_context(nc.semaphore(name))

        sel_field = sb("sel_field", [PF, FI, P], BF16)
        sel_shift = sb("sel_shift", [PF, T0 + 1, PER_TILE * FIELDS], BF16)
        sel_sum = sb("sel_sum", [PF, FIELDS], BF16)
        ident_b = sb("ident_b", [P, P], BF16)
        ident = sb("ident", [P, P])
        mask = sb("mask", [P, SB])
        row_numbers = {k: sb(f"row_numbers_{k}_sb", [P, k]) for k in sorted({k for _, k in folds})}
        w0 = sb("w0", [PER_TILE * FIELDS, T0, MAPS])
        w1_hi = sb("w1_hi", [P, FI, CUTS, MAPS], F32R)
        w1_lo = sb("w1_lo", [P, FI, CUTS, MAPS], F32R)
        w1_whole = sb("w1_whole", [P, FI, MAPS])
        w2 = sb("w2", [P, FIELDS, MAPS])
        ids = sb("ids_sb", [P, GROUPS, FIELDS], I32)
        ids_now = sb("ids_now", [P, FIELDS], I32)
        emb = sb("emb", [P, FIELDS, D])
        emb_parts = sb("emb_parts", [P, D, PF], BF16)
        x0_parts = sb("x0_parts", [PF, CHUNKS * SUBS, D, SB], BF16)
        x0_thrice = sb("x0_thrice", [PER_TILE * FIELDS, N])
        z0 = sb("z0", [PER_TILE * FIELDS, 2, N])
        x1 = sb("x1", [MAPS, N])
        x1_pat = sb("x1_pat", [P, 2, GJ, N])
        z1 = sb("z1", [P, 2, GJ - 1, N])
        z1_hi = sb("z1_hi", [P, 2, CUTS, N], F32R)
        z1_lo = sb("z1_lo", [P, 2, CUTS, N], F32R)
        x2 = sb("x2", [MAPS, SUBS, D * SB])
        x2_t = sb("x2_t", [P, SUBS, MAPS])
        x0_diag = sb("x0_diag", [P, SUBS, SB, FG])
        g_sum = sb("g_sum", [MAPS, FG, HALF + CB])
        out0 = sb("out0", [MAPS, BATCH])
        out1 = sb("out1", [MAPS, BATCH])
        out2 = sb("out2", [MAPS, BATCH])
        dense = sb("dense_sb", [P, GROUPS, D])
        bias1 = sb("bias1", [P, H1 // P])
        bias2 = sb("bias2", [P, H2 // P])
        wt3 = sb("wt3", [P, H2 // P])
        wt1 = x1_pat[:, 0, 0:3, :]
        wt1_dense = x1_pat[0:D, 0, 3, :]
        wt2 = x1_pat[:, 1, 0:2, :].rearrange("p a (k n) -> p (a k) n", k=2)
        z1_flat = z1[:, :, :, :].rearrange("p a j n -> p (a j) n")
        h1 = z1_flat[:, 0:H1 // P, :]
        h2 = z1_flat[:, H1 // P:H1 // P + H2 // P, :]
        dense_t = x1[0:D, :]
        y = x2[0:1, :, :].rearrange("o s n -> o (s n)")
        g_flat = g_sum[:, :, :].rearrange("g f b -> g (f b)")
        w1_raw = g_flat[:, 0:FI * GJ * MAPS].rearrange("p (f j m) -> p f j m", f=FI, j=GJ)
        w0_mirror = g_flat[0:PER_TILE * FIELDS, FI * GJ * MAPS:FI * GJ * MAPS + T0 * MAPS].rearrange(
            "p (t m) -> p t m", t=T0)

        x1_choice = x2[:, :, :].rearrange("p j (o q) -> p j o q", o=FQ)

        tables = z1[:, :, :, :].rearrange("p a j n -> p (a j n)")[0:small_used, 0:D * first_row[-1]].rearrange(
            "p (r d) -> p r d", d=D)
        table_parts = w2[:, :, :].bitcast(BF16).rearrange("p f m -> p (f m)")[
            0:small_used, 0:PARTS * D * first_row[-1]].rearrange("p (r k d) -> p r k d", k=PARTS, d=D)
        one_hot = x1_pat[:, :, :, :].bitcast(BF16).rearrange("p a j n -> p (a j n)")[
            0:small_used, 0:ONE_HOTS * SMALL_ROWS].rearrange("p (n k s) -> p n k s", n=ONE_HOTS, s=P)
        small_ids = x1[:, 0:FIELDS]

        pat = bank("pat", [P, 2, N])
        acc1 = bank("acc1", [MAPS, N])
        acc0 = bank("acc0", [MAPS, N])
        z1_lone = bank("z1_lone", [P, 2, N])
        misc = bank("misc", [P, 2, N])
        turned = misc[:, 0, :]
        sums = misc[:, 1, 0:SB * FG]
        tail_sums = [sums, z1_lone[:, 1, 0:SB * FG]]
        x0_t = turned[:, 0:SUBS * FIELDS].rearrange("p (s f) -> p s f", s=SUBS)
        x2t_ps = turned.rearrange("p (s m) -> p s m", s=SUBS)
        parts_t = misc[:, :, :].bitcast(BF16).rearrange("p a (d b) -> p (a d) b", b=P)
        h1_bank = [pat[:, 0, :], pat[:, 1, :], acc0[:], z1_lone[:, 0, :]]
        h2_bank = [misc[:, 0, :], misc[:, 1, :]]
        ids_bank = [pat[:, n // 4, P * (n % 4):P * (n % 4) + P] for n in range(8)] + \
                   [z1_lone[:, n // 4, P * (n % 4):P * (n % 4) + P] for n in range(8)]
        chosen = [bank_of[:, 0:len(half) * PARTS * D].rearrange("s (n k d) -> s n k d", k=PARTS, d=D)
                  for bank_of, half in zip((acc0, misc[:, 1, :]), small_halves)]
        x1_first_bank = [acc1[:], misc[:, 0, :], misc[:, 1, :], z1_lone[:, 1, :]]
        y_bank = z1_lone[0:1, 1, :]

        consts_in = sem("consts_in")
        w0_in = sem("w0_in")
        w1_in = sem("w1_in")
        w2_in = sem("w2_in")
        dense_in = sem("dense_in")
        wt1_in = sem("wt1_in")
        wt2_in = sem("wt2_in")
        small_in = sem("small_in")
        ids_in = sem("ids_in")
        ident_in = sem("ident_in")
        ids_staged = sem("ids_staged")
        rows_in = sem("rows_in")
        tables_in = [sem(f"tables_in_{h}") for h in range(2)]
        table_high = sem("table_high")
        table_rest = sem("table_rest")
        table_middle = sem("table_middle")
        table_low = sem("table_low")
        small_ids_ready = sem("small_ids_ready")
        ids_spread = sem("ids_spread")
        one_hot_ready = sem("one_hot_ready")
        chosen_ready = sem("chosen_ready")
        chosen_kept = sem("chosen_kept")
        first_parts_kept = sem("first_parts_kept")
        gathered = sem("gathered")
        split_step = sem("split_step")
        parts_turned = sem("parts_turned")
        parts_kept = sem("parts_kept")
        w0_ready = sem("w0_ready")
        w1_pad = sem("w1_pad")
        w1_hi_ready = sem("w1_hi_ready")
        w1_lo_ready = sem("w1_lo_ready")
        w1_whole_ready = sem("w1_whole_ready")
        mask_set = sem("mask_set")
        dense_turned = sem("dense_turned")
        dense_kept = sem("dense_kept")
        pat_ready = sem("pat_ready")
        thrice_ready = sem("thrice_ready")
        z0_ready = sem("z0_ready")
        l0_step = sem("l0_step")
        x1_ready = sem("x1_ready")
        choice_ready = sem("choice_ready")
        x1_first_made = sem("x1_first_made")
        x1_first_kept = sem("x1_first_kept")
        x1_stored = sem("x1_stored")
        x1_pat_in = sem("x1_pat_in")
        out0_ready = sem("out0_ready")
        z1_ready = sem("z1_ready")
        lone_ready = sem("lone_ready")
        pair_hi_ready = sem("pair_hi_ready")
        pair_lo_ready = sem("pair_lo_ready")
        lone_hi_ready = sem("lone_hi_ready")
        lone_lo_ready = sem("lone_lo_ready")
        whole_step = sem("whole_step")
        pair_high_step = sem("pair_high_step")
        pair_step = sem("pair_step")
        l1_step = sem("l1_step")
        x2_ready = sem("x2_ready")
        x2_turned = sem("x2_turned")
        x2t_ready = sem("x2t_ready")
        x0t_ready = sem("x0t_ready")
        diag_ready = sem("diag_ready")
        g_ready = sem("g_ready")
        g_kept = sem("g_kept")
        out2_done = sem("out2_done")
        out2_ready = sem("out2_ready")
        out1_ready = sem("out1_ready")
        h1_done = sem("h1_done")
        h1_ready = sem("h1_ready")
        h2_done = sem("h2_done")
        h2_ready = sem("h2_ready")
        y_done = sem("y_done")
        y_ready = sem("y_ready")
        y_out = sem("y_out")

        def at_least(eng, s, value):
            if not isinstance(value, int) or value > 0:
                eng.wait_ge(s, value)

        def is_first(c):
            return isinstance(c, int) and c == 0

        def over_chunks(eng, body, halfway):
            body(0, False, 1, 0, None)
            body(1, False, 1, 0, None)
            with eng.Fori(0, GROUPS - 2) as t:
                body(t * PER_GROUP + 2, False, t + 1, 0, t + 1)
                with eng.Fori(1, PER_GROUP) as q:
                    body(t * PER_GROUP + q + 2, False, t + 2, 0, None)
            halfway()
            body(CHUNKS - PER_GROUP - 2, False, GROUPS - 1, -HALF, GROUPS - 1)
            with eng.Fori(CHUNKS - PER_GROUP - 1, CHUNKS - 2) as c:
                body(c, False, GROUPS, -HALF, None)
            body(CHUNKS - 2, False, GROUPS, -HALF, None)
            body(CHUNKS - 1, True, GROUPS, -HALF, None)

        def shifts(i):
            return [0] if i == 0 else [t for t in (2 * i - 1, 2 * i) if t < T0]

        def order(last):
            fields = [("field", i + AHEAD) for i in range(FI - AHEAD if last else FI)]
            if last:
                return fields
            found = []
            for i, field in enumerate(fields):
                found.append(field)
                if i == 0:
                    found.append(("thrice", 0))
                found += [("shift", t) for t in shifts(i)]
            return found

        def pattern_ready(eng, c, last, what):
            n = order(last).index(what)
            at_least(eng, pat_ready, c * ITEMS + ITEMS0 + n + 1)
            return n % 2

        block = ctx.enter_context(nc.Block())

        @block.sync
        def _(sp):
            sp.dma_start(ids[:], a["ids"].rearrange("(t p) f -> p t f", p=P)).then_inc(ids_in, 16)
            sp.dma_start(ident[:], a["ident"]).then_inc(ident_in, 16)
            for k, numbers in row_numbers.items():
                sp.dma_start(numbers[:], a[f"row_numbers_{k}"]).then_inc(rows_in, 16)
            for dst, name in ((ident_b, "ident_b"), (sel_shift, "sel_shift"), (sel_field, "sel_field"),
                              (sel_sum, "sel_sum"), (mask, "mask")):
                sp.dma_start(dst[:], a[name]).then_inc(consts_in, 16)
            sp.dma_start(w0[:], a["w0_upper"]).then_inc(w0_in, 16)
            sp.dma_start(w0_mirror, a["w0_lower"]).then_inc(w0_in, 16)
            sp.dma_start(dense[:], a["dense_ctx"].rearrange("(t p) d -> p t d", p=P)).then_inc(dense_in, 16)
            for h, half in enumerate(small_halves):
                sp.wait_ge(tables_in[h], 16 * len(half))
            for fq in range(FQ):
                fields = min(FI, FIELDS - FI * fq)
                sp.dma_start(w1_raw[32 * fq:32 * fq + 32, 0:fields, :, :].rearrange("p f j m -> p f (j m)"),
                             w1_rows[FI * fq:FI * fq + fields, :, :].rearrange("f q n -> q f n")).then_inc(w1_in, 16)
            with nc.allow_non_contiguous_dma(reason="a few hundred words"):
                sp.dma_start(bias1[:], a["b_top1"].rearrange("(k p) -> p k", p=P)).then_inc(small_in, 16)
                sp.dma_start(bias2[:], a["b_top2"].rearrange("(k p) -> p k", p=P)).then_inc(small_in, 16)
                sp.dma_start(wt3[:], a["W_top3"].rearrange("(k p) o -> p (k o)", p=P)).then_inc(small_in, 16)

            sp.wait_ge(chosen_ready, len(small))
            sp.dma_start(w2[:], w2_rows).then_inc(w2_in, 16)

            def spread(c):
                at_least(sp, x1_ready, c + 1)
                sp.dma_start(x1_dram[c], x1[:]).then_inc(x1_stored, 16)
                at_least(sp, x1_stored, 16 * c)
                if not (isinstance(c, int) and c == 1):
                    at_least(sp, z1_ready, FI * c - FI)
                for fq in range(FQ):
                    sp.dma_start(x1_pat[32 * fq:32 * fq + 32, c % 2, :, :].rearrange("q j n -> q (j n)"),
                                 x1_dram[c].rearrange("(q j) n -> q (j n)", j=GJ)).then_inc(x1_pat_in, 16)

            spread(1)
            with sp.Fori(2, CHUNKS) as c:
                spread(c)
            sp.wait_ge(z1_ready, FI * (CHUNKS - 1))
            sp.dma_start(wt1, a["W_top1"][0:3 * MAPS, :].rearrange("(k p) n -> p k n", p=P)).then_inc(wt1_in, 16)
            sp.dma_start(wt1_dense, a["W_top1"][3 * MAPS:3 * MAPS + D, :]).then_inc(wt1_in, 16)
            sp.wait_ge(z1_ready, FI * CHUNKS)
            sp.dma_start(wt2, a["W_top2"].rearrange("(k p) n -> p k n", p=P)).then_inc(wt2_in, 16)
            sp.wait_ge(y_ready, 1)
            sp.dma_start(a["out"].rearrange("b o -> o b"), y).then_inc(y_out, 16)
            sp.wait_ge(y_out, 16)

        @block.gpsimd
        def _(pool):
            def stage_ids(t):
                if not is_first(t):
                    pool.wait_ge(gathered, t * (16 * FIELDS) - 16 * len(small))
                pool.tensor_copy(ids_now[:], ids[:, bass.ds(t, 1), :].rearrange("p o f -> p (o f)")).then_inc(ids_staged, 1)
                at_least(pool, ids_staged, t + 1)
                at_least(pool, split_step, t * 4)

            def gather(fields):
                for f in fields:
                    pool.indirect_dma_start(
                        out=emb[:, f, :], out_offset=None, in_=a[f"tbl_{f}"][:, :],
                        in_offset=bass.IndirectOffsetOnAxis(ap=ids_now[:, f:f + 1], axis=0),
                    ).then_inc(gathered, 16)

            def cut_pair(c, i):
                at_least(pool, pair_hi_ready, c * FI + i + 1)
                if not (is_first(c) and i < 2):
                    at_least(pool, pair_step, c * FI + (i - 1))
                pool.tensor_tensor(z1_lo[:, i % 2, 1:3, :], z1[:, i % 2, 0:2, :],
                                   z1_hi[:, i % 2, 1:3, :].bitcast(F32), ALU.subtract).then_inc(pair_lo_ready, 1)

            def body(c, last, fields):
                for i in range(FI):
                    if i + AHEAD < FI:
                        cut_pair(c, i + AHEAD)
                    elif not last:
                        cut_pair(c + 1, i + AHEAD - FI)
                    share = (2, 3, 3, 3, 0, 0, 1, 0, 1, 1)[i]
                    gather(fields[:share])
                    fields = fields[share:]

            def part_of(fields, q, n):
                size = -(-len(fields) // n)
                return fields[size * q:size * q + size]

            pool.wait_ge(ids_in, 16)
            stage_ids(0)
            gather(large)
            pool.wait_ge(w1_hi_ready, 1)
            pool.tensor_tensor(w1_lo[:], w1_raw[:, :, 0:CUTS, :], w1_hi[:].bitcast(F32),
                               ALU.subtract).then_inc(w1_lo_ready, 1)
            stage_ids(1)
            gather(range(FIRST_GATHERS))
            for i in range(AHEAD):
                cut_pair(0, i)
            for c in range(2):
                body(c, False, part_of(range(FIRST_GATHERS, FIELDS), c, 2))
            with pool.Fori(0, GROUPS - 2) as t:
                body(t * PER_GROUP + 2, False, [])
                stage_ids(t + 2)
                for q in range(1, PER_GROUP):
                    body(t * PER_GROUP + q + 2, False, part_of(range(FIELDS), q - 1, PER_GROUP - 1))
            with pool.Fori(CHUNKS - PER_GROUP - 2, CHUNKS - 2) as c:
                body(c, False, [])
            body(CHUNKS - 2, False, [])
            body(CHUNKS - 1, True, [])

        @block.vector
        def _(dve):
            def cut_embeddings(t, k):
                value = emb[:, :, :].rearrange("p f d -> p d f")
                part = [emb_parts[:, :, FIELDS * j:FIELDS * j + FIELDS] for j in range(PARTS)]
                if k == 0:
                    at_least(dve, gathered, t * (16 * FIELDS) + 16 * len(large))
                    at_least(dve, parts_turned, t)
                    dve.tensor_copy(part[0], value).then_inc(split_step, 1)
                elif k == 1:
                    at_least(dve, split_step, t * 4 + 1)
                    dve.tensor_tensor(value, value, part[0], ALU.subtract).then_inc(split_step, 1)
                elif k == 2:
                    at_least(dve, split_step, t * 4 + 2)
                    dve.tensor_copy(part[1], value).then_inc(split_step, 1)
                else:
                    at_least(dve, split_step, t * 4 + 3)
                    dve.tensor_tensor(part[2], value, part[1], ALU.subtract).then_inc(split_step, 1)

            dve.memset(w1_raw[32 * (FQ - 1):P, FI - 1, :, :], 0.0).then_inc(w1_pad, 1)
            dve.wait_ge(ids_in, 16)
            dve.tensor_copy(small_ids, ids[:, 0, :]).then_inc(small_ids_ready, 1)
            dve.wait_ge(rows_in, 16 * len(row_numbers))

            def one_hot_rows(n):
                k = folds[n][1]
                dve.wait_ge(ids_spread, min(4 * (n // 4) + 4, len(small)))
                if n >= ONE_HOTS:
                    dve.wait_ge(chosen_ready, n - ONE_HOTS + 1)
                dve.tensor_tensor(
                    one_hot[:, n % ONE_HOTS, 0:k, :],
                    ids_bank[n][0:small_used, :].rearrange("p (o s) -> p o s", o=1).to_broadcast([small_used, k, P]),
                    row_numbers[k][0:small_used, :].rearrange("p (k o) -> p k o", o=1).to_broadcast([small_used, k, P]),
                    ALU.is_equal).then_inc(one_hot_ready, 1)

            def table_less_high(h):
                rows = slice(first_row[half_of[h]], first_row[half_of[h + 1]])
                dve.wait_ge(table_high, h + 1)
                dve.tensor_tensor(tables[:, rows, :], tables[:, rows, :], table_parts[:, rows, 0, :],
                                  ALU.subtract).then_inc(table_rest, 1)

            def table_less_middle(h):
                rows = slice(first_row[half_of[h]], first_row[half_of[h + 1]])
                dve.wait_ge(table_middle, h + 1)
                dve.wait_ge(table_rest, h + 1)
                dve.tensor_tensor(table_parts[:, rows, 2, :], tables[:, rows, :], table_parts[:, rows, 1, :],
                                  ALU.subtract).then_inc(table_low, 1)

            for n in range(ONE_HOTS):
                one_hot_rows(n)
            table_less_high(0)
            table_less_high(1)
            table_less_middle(0)
            table_less_middle(1)
            for n in range(ONE_HOTS, len(small)):
                one_hot_rows(n)
            dve.wait_ge(consts_in, 80)
            dve.tensor_copy(x0_diag[:, :, :, FIELDS], mask[:].rearrange("p (o b) -> p o b", o=1)
                            .to_broadcast([P, SUBS, SB])).then_inc(mask_set, 1)
            for j in range(GJ):
                dve.tensor_copy(x1_choice[:, j, :, :], ident[:].rearrange("p (o q j) -> p j o q", o=1, j=GJ)[:, j, :, :]
                                .to_broadcast([P, FQ, GQ])).then_inc(choice_ready, 1)
            dve.wait_ge(w0_in, 32)
            dve.tensor_tensor(w0[:], w0[:], w0_mirror, ALU.add).then_inc(w0_ready, 1)
            kept = 0
            for h, half in enumerate(small_halves):
                dve.wait_ge(chosen_ready, half_of[h + 1])
                for n, f, count in runs([small[n] for n in half]):
                    dve.tensor_reduce(emb[:, f:f + count, :],
                                      chosen[h][:, n:n + count, :, :].rearrange("s n k d -> s n d k"),
                                      AX_X, ALU.add).then_inc(chosen_kept, 1)
                    kept += 1
            dve.wait_ge(chosen_kept, kept)
            for k in range(4):
                cut_embeddings(0, k)

            def products0(c, t, bank_of):
                rows = tile_rows(t)
                if t == 0:
                    at_least(dve, thrice_ready, c + 1)
                if not (isinstance(c, int) and c == 0 and t < 2):
                    at_least(dve, l0_step, c * T0 + max(t - 1, 0))
                dve.tensor_tensor(z0[0:rows, t % 2, :], pat[0:rows, bank_of, :], x0_thrice[0:rows, :],
                                  ALU.mult).then_inc(z0_ready, 1)

            def products1(c, i, bank_of):
                early = is_first(c) and i < 2
                first = i == 0 and is_first(c)
                if first:
                    dve.wait_ge(x1_first_kept, 1)
                elif i == 0:
                    at_least(dve, x1_pat_in, c * (16 * FQ))
                if not early:
                    at_least(dve, lone_lo_ready, c * FI + (i - 1))
                dve.tensor_tensor(z1_lone[:, i % 2, :], pat[:, bank_of, :], x1_pat[:, c % 2, LONE, :],
                                  ALU.mult).then_inc(lone_ready, 1)
                if not early:
                    at_least(dve, pair_lo_ready, c * FI + (i - 1))
                    at_least(dve, whole_step, c * FI + (i - 1))
                if first:
                    dve.wait_ge(x1_first_kept, GJ)
                dve.tensor_tensor(z1[:, i % 2, :, :], pat[:, bank_of:bank_of + 1, :].to_broadcast([P, GJ - 1, N]),
                                  x1_pat[:, c % 2, PAIR[0]:WHOLE + 1, :], ALU.mult).then_inc(z1_ready, 1)

            def cut_lone(c, i):
                at_least(dve, lone_hi_ready, c * FI + i + 1)
                if not (is_first(c) and i < 2):
                    at_least(dve, l1_step, c * FI + (i - 1))
                dve.tensor_tensor(z1_lo[:, i % 2, LONE, :], z1_lone[:, i % 2, :],
                                  z1_hi[:, i % 2, LONE, :].bitcast(F32), ALU.subtract).then_inc(lone_lo_ready, 1)

            def sum_x1(c):
                at_least(dve, x1_ready, c + 1)
                dve.tensor_reduce(out0[:, bass.ds(c * CB, CB)].rearrange("m (s b) -> m s b", s=SUBS),
                                  x1[:].rearrange("m (s d b) -> m s b d", s=SUBS, d=D),
                                  AX_X, ALU.add).then_inc(out0_ready, 1)

            def diagonal(c, s):
                if s == 0:
                    at_least(dve, x0t_ready, c + 1)
                    at_least(dve, g_ready, c * SUBS)
                dve.tensor_tensor(
                    x0_diag[:, s, :, 0:FIELDS], x0_t[:, s:s + 1, :].to_broadcast([P, SB, FIELDS]),
                    mask[:].rearrange("p (b o) -> p b o", o=1).to_broadcast([P, SB, FIELDS]),
                    ALU.mult).then_inc(diag_ready, 1)

            for t in range(T0):
                dve.wait_ge(pat_ready, t + 2)
                products0(0, t, (t + 1) % 2)
            for i in range(AHEAD):
                dve.wait_ge(pat_ready, T0 + 2 + i)
                products1(0, i, (T0 + 1 + i) % 2)
            sum_x1(0)
            cut_lone(0, 0)

            def body(c, last, groups, place, group):
                for i in range(FI):
                    if not is_first(c):
                        for s in range(SUBS) if i == 4 else []:
                            diagonal(c - 1, s)
                    if i + AHEAD < FI:
                        products1(c, i + AHEAD, pattern_ready(dve, c, last, ("field", i + AHEAD)))
                    elif not last:
                        products1(c + 1, i + AHEAD - FI, pattern_ready(dve, c, last, ("field", i + AHEAD)))
                    now = [] if last else shifts(i)
                    if len(now) == 2:
                        products0(c + 1, now[0], pattern_ready(dve, c, last, ("shift", now[0])))
                    if i + 1 < FI:
                        cut_lone(c, i + 1)
                    elif not last:
                        cut_lone(c + 1, 0)
                    for t in now[-1:]:
                        products0(c + 1, t, pattern_ready(dve, c, last, ("shift", t)))
                    if group is not None and 1 <= i < 5:
                        cut_embeddings(group, i - 1)
                    if i == 6 and not last:
                        sum_x1(c + 1)

            over_chunks(dve, body, lambda: None)
            for s in range(SUBS):
                diagonal(CHUNKS - 1, s)
            dve.wait_ge(dense_turned, 1)
            dve.wait_ge(x1_stored, 16 * (CHUNKS - 1))
            dve.wait_ge(out0_ready, CHUNKS)
            dve.tensor_copy(dense_t, pat[0:D, 0, :]).then_inc(dense_kept, 1)

        @block.scalar
        def _(act):
            def keep_parts(t):
                at_least(act, parts_turned, t + 1)
                act.copy(x0_parts[:, bass.ds(t * (PER_GROUP * SUBS), PER_GROUP * SUBS), :, :],
                         parts_t[0:PF, :, :].rearrange("r d (s b) -> r s d b", b=SB)).then_inc(parts_kept, 1)

            def keep_thrice(c, bank_of):
                at_least(act, z0_ready, c * T0)
                act.copy(x0_thrice[:], pat[0:PER_TILE * FIELDS, bank_of, :]).then_inc(thrice_ready, 1)

            def keep_x1(c):
                at_least(act, l0_step, c * T0 + T0)
                at_least(act, x1_stored, c * 16 - 16)
                at_least(act, out0_ready, c)
                act.copy(x1[:], acc0[:]).then_inc(x1_ready, 1)

            def keep_x2(c):
                at_least(act, l1_step, c * FI + FI)
                at_least(act, x2_turned, c)
                act.copy(x2[:], acc1[:].rearrange("m (s n) -> m s n", s=SUBS)).then_inc(x2_ready, 1)

            def keep_x2_t(c):
                at_least(act, x2_turned, c + 1)
                at_least(act, g_ready, c * SUBS)
                act.copy(x2_t[:], x2t_ps).then_inc(x2t_ready, 1)

            def keep_g(c, s, place, bank_of=sums):
                at_least(act, g_ready, c * SUBS + s + 1)
                act.copy(g_sum[:, :, bass.ds(c * CB + (s * SB + place), SB)],
                         bank_of.rearrange("g (b f) -> g f b", b=SB)).then_inc(g_kept, 1)

            def high_pair(c, i):
                at_least(act, z1_ready, c * FI + i + 1)
                if not (is_first(c) and i < 2):
                    at_least(act, pair_high_step, c * FI + (i - 1))
                    at_least(act, pair_lo_ready, c * FI + (i - 1))
                act.copy(z1_hi[:, i % 2, 1:3, :], z1[:, i % 2, 0:2, :]).then_inc(pair_hi_ready, 1)

            def high_lone(c, i):
                at_least(act, lone_ready, c * FI + i + 1)
                if not (is_first(c) and i < 2):
                    at_least(act, l1_step, c * FI + (i - 1))
                act.copy(z1_hi[:, i % 2, LONE, :], z1_lone[:, i % 2, :]).then_inc(lone_hi_ready, 1)

            for h, half in enumerate(small_halves):
                for n in half:
                    act.dma_start(tables[:, first_row[n]:first_row[n + 1], :].rearrange("p r d -> p (r d)"),
                                  a[f"tbl_{small[n]}"].rearrange("(p r) d -> p (r d)", p=small_used)).then_inc(tables_in[h], 16)
            for h, half in enumerate(small_halves):
                rows = slice(first_row[half_of[h]], first_row[half_of[h + 1]])
                act.wait_ge(tables_in[h], 16 * len(half))
                act.copy(table_parts[:, rows, 0, :], tables[:, rows, :]).then_inc(table_high, 1)
            for h in range(2):
                rows = slice(first_row[half_of[h]], first_row[half_of[h + 1]])
                act.wait_ge(table_rest, h + 1)
                act.copy(table_parts[:, rows, 1, :], tables[:, rows, :]).then_inc(table_middle, 1)
            act.wait_ge(w1_in, 16 * FQ)
            act.wait_ge(w1_pad, 1)
            act.copy(w1_hi[:], w1_raw[:, :, 0:CUTS, :]).then_inc(w1_hi_ready, 1)
            act.copy(w1_whole[:], w1_raw[:, :, WHOLE, :]).then_inc(w1_whole_ready, 1)
            act.wait_ge(parts_turned, 1)
            act.copy(x0_parts[:, 0:SUBS, :, :],
                     parts_t[0:PF, :, 0:CB].rearrange("r d (s b) -> r s d b", b=SB)).then_inc(first_parts_kept, 1)
            act.wait_ge(pat_ready, 1)
            keep_thrice(0, 0)
            act.copy(x0_parts[:, SUBS:PER_GROUP * SUBS, :, :],
                     parts_t[0:PF, :, CB:P].rearrange("r d (s b) -> r s d b", b=SB)).then_inc(parts_kept, 1)
            keep_x1(0)
            for j in range(GJ):
                act.wait_ge(x1_first_made, j + 1)
                act.copy(x1_pat[:, 0, j, :], x1_first_bank[j]).then_inc(x1_first_kept, 1)
            high_lone(0, 0)
            for i in range(AHEAD):
                high_pair(0, i)

            def body(c, last, groups, place, group):
                for i in range(FI):
                    if i == 0 and not last:
                        keep_thrice(c + 1, pattern_ready(act, c, last, ("thrice", 0)))
                    if i + 1 < FI:
                        high_lone(c, i + 1)
                    elif not last:
                        high_lone(c + 1, 0)
                    if i == FI - 1:
                        keep_x2(c)
                    if i + AHEAD < FI:
                        high_pair(c, i + AHEAD)
                    elif not last:
                        high_pair(c + 1, i + AHEAD - FI)
                    if i == 4 and not is_first(c):
                        keep_x2_t(c - 1)
                    if i == 4 and not last:
                        keep_x1(c + 1)
                    if i == 5 and group is not None:
                        keep_parts(group)
                    if i - 6 in range(SUBS) and not is_first(c):
                        keep_g(c - 1, i - 6, place)

            def halfway():
                act.copy(out1[:, 0:HALF], g_sum[:, FIELDS, 0:HALF]).then_inc(out1_ready, 1)
                act.wait_ge(out1_ready, 1)
                act.wait_ge(out2_done, 1)
                act.copy(out2[:, 0:HALF], acc0[:, 0:HALF]).then_inc(out2_ready, 1)

            over_chunks(act, body, halfway)
            keep_x2_t(CHUNKS - 1)
            for s in range(SUBS):
                keep_g(CHUNKS - 1, s, -HALF, tail_sums[s % 2])
            act.wait_ge(g_kept, CHUNKS * SUBS)
            act.copy(out1[:, HALF + CB:BATCH], g_sum[:, FIELDS, CB:HALF]).then_inc(out1_ready, 1)
            act.copy(out1[:, HALF:HALF + CB], g_sum[:, FIELDS, HALF:HALF + CB]).then_inc(out1_ready, 1)
            act.wait_ge(out2_done, 2)
            act.copy(out2[:, HALF + CB:BATCH], acc1[:, 0:HALF - CB]).then_inc(out2_ready, 1)
            act.copy(out2[:, HALF:HALF + CB], acc1[:, HALF - CB:HALF]).then_inc(out2_ready, 1)
            act.wait_ge(small_in, 48)
            for m in range(H1 // P):
                act.wait_ge(h1_done, m + 1)
                act.activation(h1[:, m, :], h1_bank[m], ACT.Relu, bias=bias1[:, m:m + 1]).then_inc(h1_ready, 1)
            for m in range(H2 // P):
                act.wait_ge(h2_done, m + 1)
                act.activation(h2[:, m, :], h2_bank[m], ACT.Relu, bias=bias2[:, m:m + 1]).then_inc(h2_ready, 1)
            act.wait_ge(y_done, 1)
            act.copy(y, y_bank).then_inc(y_ready, 1)

        @block.tensor
        def _(pe):
            def turn_parts(t):
                at_least(pe, split_step, t * 4 + 4)
                if not is_first(t):
                    at_least(pe, g_kept, t * (PER_GROUP * SUBS) - (PER_GROUP - 1) * SUBS)
                    at_least(pe, x2t_ready, t * PER_GROUP - (PER_GROUP - 2))
                for d in range(D):
                    last = pe.transpose(parts_t[0:PF, d, :], emb_parts[:, d, :], ident_b[:])
                last.then_inc(parts_turned, 1)

            def parts(c):
                return x0_parts[:, bass.ds(c * SUBS, SUBS), :, :].rearrange("r s d b -> r (s d b)")

            def pattern(sel, c, bank_of):
                pe.matmul(pat[0:sel.shape[1], bank_of, :], sel, parts(c), start=True, stop=True).then_inc(pat_ready, 1)

            def body_pattern(c, last, what):
                n = order(last).index(what)
                if n >= 2:
                    before, k = order(last)[n - 2]
                    if before == "field":
                        at_least(pe, z1_ready, c * FI + k + 1)
                    elif before == "thrice":
                        at_least(pe, thrice_ready, c + 2)
                    else:
                        at_least(pe, z0_ready, c * T0 + (T0 + k + 1))
                else:
                    at_least(pe, z1_ready, c * FI + n + 1)
                kind, k = what
                if kind == "field":
                    pattern(sel_field[:, k % FI, :], c + k // FI, n % 2)
                elif kind == "thrice":
                    pattern(sel_shift[:, T0, :], c + 1, n % 2)
                else:
                    pattern(sel_shift[:, k, 0:tile_rows(k)], c + 1, n % 2)

            def layer0(c, t, halves=0):
                at_least(pe, z0_ready, c * T0 + t + 1)
                if t == 0:
                    at_least(pe, x1_ready, c)
                    if halves:
                        at_least(pe, out2_ready, halves)
                rows = tile_rows(t)
                pe.matmul(acc0[:], w0[0:rows, t, :], z0[0:rows, t % 2, :],
                          start=(t == 0), stop=(t == T0 - 1)).then_inc(l0_step, 1)

            def layer1_whole(c, i):
                at_least(pe, z1_ready, c * FI + i + 1)
                if i == 0:
                    at_least(pe, x2_ready, c)
                pe.matmul(acc1[:], w1_whole[:, i, :], z1[:, i % 2, 2, :],
                          start=(i == 0), stop=False).then_inc(whole_step, 1)

            def layer1_high(i, j):
                pe.matmul(acc1[:], w1_hi[:, i, j, :], z1_hi[:, i % 2, j, :], start=False, stop=False)
                return pe.matmul(acc1[:], w1_lo[:, i, j, :], z1_hi[:, i % 2, j, :], start=False, stop=False)

            def layer1_low(i, j, stop=False):
                return pe.matmul(acc1[:], w1_hi[:, i, j, :], z1_lo[:, i % 2, j, :], start=False, stop=stop)

            def layer1_pair_high(c, i, j):
                if j == PAIR[0]:
                    at_least(pe, pair_hi_ready, c * FI + i + 1)
                last = layer1_high(i, j)
                if j == PAIR[-1]:
                    last.then_inc(pair_high_step, 1)

            def layer1_pair_low(c, i):
                at_least(pe, pair_lo_ready, c * FI + i + 1)
                for j in PAIR:
                    last = layer1_low(i, j)
                last.then_inc(pair_step, 1)

            def layer1_lone(c, i):
                at_least(pe, lone_hi_ready, c * FI + i + 1)
                layer1_high(i, LONE)
                at_least(pe, lone_lo_ready, c * FI + i + 1)
                layer1_low(i, LONE, stop=(i == FI - 1)).then_inc(l1_step, 1)

            def turn_x0(c):
                at_least(pe, x2t_ready, c)
                for s in range(SUBS):
                    last = pe.matmul(x0_t[:, s, :],
                                     x0_parts[:, bass.ds(c * SUBS + s, 1), :, :].rearrange("r o d b -> r (o d b)"),
                                     sel_sum[:], start=True, stop=True)
                last.then_inc(x0t_ready, 1)

            def turn_x2(c):
                at_least(pe, x2_ready, c + 1)
                at_least(pe, diag_ready, c * SUBS + SUBS)
                for s in range(SUBS):
                    last = pe.transpose(x2t_ps[:, s, :], x2[:, s, :], ident[:])
                last.then_inc(x2_turned, 1)

            def sum_products(c, s, kept, into):
                if s == 0:
                    at_least(pe, x2t_ready, c + 1)
                at_least(pe, g_kept, kept)
                pe.matmul(into, x2_t[:, s, :],
                          x0_diag[:, s, :, :].rearrange("p b f -> p (b f)"), start=True, stop=True).then_inc(g_ready, 1)

            def layer2(acc, first):
                for f in range(FIELDS):
                    last = pe.matmul(acc[:, 0:HALF], w2[:, f, :], g_sum[:, f, first:first + HALF],
                                     start=(f == 0), stop=(f == FIELDS - 1))
                last.then_inc(out2_done, 1)

            pe.wait_ge(ident_in, 16)
            pe.wait_ge(small_ids_ready, 1)
            for n, f in enumerate(small):
                pe.matmul(ids_bank[n], small_ids[:, f:f + 1].to_broadcast([P, P]), ident[:],
                          start=True, stop=True).then_inc(ids_spread, 1)
            for h, half in enumerate(small_halves):
                pe.wait_ge(table_low, h + 1)
                for n in half:
                    k = folds[n][1]
                    pe.wait_ge(one_hot_ready, n + 1)
                    for j in range(k):
                        last = pe.matmul(chosen[h][:, n - half_of[h], :, :].rearrange("s k d -> s (k d)"),
                                         one_hot[:, n % ONE_HOTS, j, :],
                                         table_parts[:, first_row[n] + j, :, :].rearrange("p k d -> p (k d)"),
                                         start=(j == 0), stop=(j == k - 1))
                    last.then_inc(chosen_ready, 1)

            pe.wait_ge(consts_in, 80)
            turn_parts(0)
            pe.wait_ge(first_parts_kept, 1)
            pattern(sel_shift[:, T0, :], 0, 0)
            pe.wait_ge(w0_ready, 1)
            for t in range(T0):
                if t == 1:
                    pe.wait_ge(thrice_ready, 1)
                elif t >= 2:
                    pe.wait_ge(z0_ready, t - 1)
                pattern(sel_shift[:, t, 0:tile_rows(t)], 0, (t + 1) % 2)
                if t >= 1:
                    layer0(0, t - 1)
            for i in range(AHEAD):
                pe.wait_ge(z0_ready, T0 - 1 + i)
                if i == 0:
                    pattern(sel_field[:, i, :], 0, (T0 + 1 + i) % 2)
                    layer0(0, T0 - 1)
                else:
                    pattern(sel_field[:, i, :], 0, (T0 + 1 + i) % 2)
            pe.wait_ge(choice_ready, GJ)
            pe.wait_ge(parts_kept, 1)
            pe.wait_ge(x1_ready, 1)
            for j in range(GJ):
                pe.matmul(x1_first_bank[j], x1_choice[:, j, :, :].rearrange("p o q -> p (o q)"), x1[:], start=True, stop=True).then_inc(x1_first_made, 1)
            pe.wait_ge(w1_whole_ready, 1)
            pe.wait_ge(w1_hi_ready, 1)
            pe.wait_ge(w1_lo_ready, 1)
            pe.wait_ge(mask_set, 1)

            def body(c, last, groups, place, group):
                for i in range(FI):
                    if i + AHEAD < FI or not last:
                        body_pattern(c, last, ("field", i + AHEAD))
                    if i == 0:
                        at_least(pe, parts_kept, groups)
                        if not last:
                            body_pattern(c, last, ("thrice", 0))
                        if not is_first(c):
                            turn_x0(c - 1)
                    layer1_whole(c, i)
                    now = [] if last else shifts(i)
                    before = [] if last or i == 0 else shifts(i - 1)
                    if i > 1:
                        for t in before:
                            layer0(c + 1, t)
                    layer1_pair_high(c, i, PAIR[0])
                    if len(now) == 2:
                        body_pattern(c, last, ("shift", now[0]))
                    layer1_pair_high(c, i, PAIR[1])
                    if i == 1 and not last:
                        layer0(c + 1, 0, halves=1 if place else 0)
                    layer1_pair_low(c, i)
                    if i == 5 and group is not None:
                        turn_parts(group)
                    if len(now) == 2:
                        body_pattern(c, last, ("shift", now[1]))
                    layer1_lone(c, i)
                    if len(now) == 1:
                        body_pattern(c, last, ("shift", now[0]))
                    if i == 4 and not is_first(c):
                        turn_x2(c - 1)
                    if i - 6 in range(SUBS) and not is_first(c):
                        if i == 6 and group is not None:
                            at_least(pe, parts_kept, group + 1)
                        sum_products(c - 1, i - 6, (c - 1) * SUBS + (i - 6), sums)

            def halfway():
                pe.wait_ge(w2_in, 16)
                pe.wait_ge(g_kept, CHUNKS // 2 * SUBS)
                layer2(acc0, 0)

            over_chunks(pe, body, halfway)

            turn_x0(CHUNKS - 1)
            pe.wait_ge(dense_in, 16)
            for t in range(GROUPS):
                last = pe.transpose(pat[0:D, 0, P * t:P * t + P], dense[:, t, :], ident[:])
            last.then_inc(dense_turned, 1)
            pe.wait_ge(wt1_in, 32)
            pe.wait_ge(out0_ready, CHUNKS)

            def top1_out0(m):
                pe.matmul(h1_bank[m], wt1[:, 0, P * m:P * m + P], out0[:], start=True, stop=False)

            def top1_dense(m):
                pe.matmul(h1_bank[m], wt1_dense[:, P * m:P * m + P], dense_t, start=False, stop=False)

            for m in range(1, H1 // P):
                top1_out0(m)
            turn_x2(CHUNKS - 1)
            pe.wait_ge(dense_kept, 1)
            top1_dense(1)
            top1_dense(2)
            before = (CHUNKS - 1) * SUBS
            sum_products(CHUNKS - 1, 0, before, tail_sums[0])
            sum_products(CHUNKS - 1, 1, before, tail_sums[1])
            top1_out0(0)
            sum_products(CHUNKS - 1, 2, before + 1, tail_sums[0])
            top1_dense(0)
            sum_products(CHUNKS - 1, 3, before + 2, tail_sums[1])
            top1_dense(3)
            pe.wait_ge(g_kept, CHUNKS * SUBS)
            layer2(acc1, CB)

            pe.wait_ge(out1_ready, 3)
            for m in range(H1 // P):
                pe.matmul(h1_bank[m], wt1[:, 1, P * m:P * m + P], out1[:], start=False, stop=False)
            pe.wait_ge(out2_ready, 3)
            for m in range(H1 // P):
                pe.matmul(h1_bank[m], wt1[:, 2, P * m:P * m + P], out2[:], start=False, stop=True).then_inc(h1_done, 1)
            pe.wait_ge(wt2_in, 16)
            for k in range(H1 // P):
                pe.wait_ge(h1_ready, k + 1)
                for m in range(H2 // P):
                    mm = pe.matmul(h2_bank[m], wt2[:, k, P * m:P * m + P], h1[:, k, :],
                                   start=(k == 0), stop=(k == H1 // P - 1))
                    if k == H1 // P - 1:
                        mm.then_inc(h2_done, 1)
            pe.wait_ge(small_in, 48)
            for k in range(H2 // P):
                pe.wait_ge(h2_ready, k + 1)
                last = pe.matmul(y_bank, wt3[:, k:k + 1], h2[:, k, :], start=(k == 0), stop=(k == H2 // P - 1))
            last.then_inc(y_done, 1)


def selectors():
    field = np.zeros((PARTS, FIELDS, FI, P), np.float32)
    for i in range(FI):
        for row in range(P):
            f = FI * (row // GQ) + i
            if f < FIELDS:
                field[:, f, i, row] = 1
    shift = np.zeros((PARTS, FIELDS, T0 + 1, PER_TILE, FIELDS), np.float32)
    for g in range(FIELDS):
        for u in range(PER_TILE):
            shift[:, g, T0, u, g] = 1
            for t in range(T0):
                shift[:, (g + PER_TILE * t + u) % FIELDS, t, u, g] = 1
    total = np.zeros((PARTS, FIELDS, FIELDS), np.float32)
    total[:, np.arange(FIELDS), np.arange(FIELDS)] = 1
    return (field.reshape(PF, FI, P), shift.reshape(PF, T0 + 1, PER_TILE * FIELDS), total.reshape(PF, FIELDS))


def shift_rows():
    upper = np.full((PER_TILE * FIELDS, T0), -1)
    lower = np.full((PER_TILE * FIELDS, T0), -1)
    for s in range(SHIFTS):
        for g in range(FIELDS):
            row, t, h = FIELDS * (s % PER_TILE) + g, s // PER_TILE, (g + s) % FIELDS
            upper[row, t] = g * FIELDS + h
            if s:
                lower[row, t] = h * FIELDS + g
    return upper, lower


def kernel(**inputs):
    import concourse.bacc as bacc
    import ml_dtypes
    from concourse.bass_utils import run_bass_kernel_spmd

    arrays = {name: np.ascontiguousarray(value) for name, value in inputs.items()}
    bf16 = np.dtype(ml_dtypes.bfloat16)
    field, shift, total = selectors()
    arrays["sel_field"], arrays["sel_shift"], arrays["sel_sum"] = field.astype(bf16), shift.astype(bf16), total.astype(bf16)
    arrays["ident"] = np.eye(P, dtype=np.float32)
    arrays["ident_b"] = np.eye(P, dtype=np.float32).astype(bf16)
    arrays["mask"] = np.tile(np.eye(SB, dtype=np.float32), (P // SB, 1))
    for k in {fold(len(arrays[f"tbl_{f}"]))[1] for f in range(FIELDS)}:
        if k <= SMALL_ROWS // P:
            arrays[f"row_numbers_{k}"] = np.arange(P * k, dtype=np.float32).reshape(P, k)
    w0_rows = arrays.pop("L0_rec_f0")
    for name, rows in zip(("w0_upper", "w0_lower"), shift_rows()):
        laid = np.zeros((*rows.shape, MAPS), w0_rows.dtype)
        laid[rows >= 0] = w0_rows[rows[rows >= 0]]
        arrays[name] = laid

    nc = bacc.Bacc("TRN2", target_bir_lowering=False, num_devices=1)
    a = {name: nc.dram_tensor(f"in_{name}", value.shape, mybir.dt.from_np(value.dtype), kind="ExternalInput").ap()
         for name, value in arrays.items()}
    a["out"] = nc.dram_tensor("out_y", (BATCH, 1), F32, kind="ExternalOutput").ap()
    build_program(nc, a)
    result = run_bass_kernel_spmd(nc, [{f"in_{name}": value for name, value in arrays.items()}], core_ids=[0])
    return result.results[0]["out_y"]
```
